# Optimizing a Trainium2 kernel written in Bass

```python
import numpy as np
import jax
import jax.numpy as jnp

def _softmax(x, axis=-1):
    return jax.nn.softmax(x, axis=axis)

def _gelu(x):
    return jax.nn.gelu(x, approximate=True)

def _silu(x):
    return jax.nn.silu(x)

def _sigmoid(x):
    return jax.nn.sigmoid(x)

def _layernorm(x, axis=-1, eps=1e-05):
    m = jnp.mean(x, axis=axis, keepdims=True)
    v = jnp.var(x, axis=axis, keepdims=True)
    return (x - m) / jnp.sqrt(v + eps)

def _scatter_add(tgt, idx, src, axis=0):
    return tgt.at[idx].add(src)

def _segment_sum(src, seg, n):
    return jax.ops.segment_sum(src, seg, n)
kernel_name = 'mk_gnn_preln_d1_gnn_r8_bfa7a0'

def setup_inputs(seed: int=0):
    np.random.seed(seed)
    _w = jnp.asarray

    def _rec_inputs():
        import jax
        import jax.numpy as jnp
        _gk = jax.random.key(seed)
        x = 0.0001712 + 1 * jax.random.normal(jax.random.fold_in(_gk, 1), (12500, 16), jnp.float32)
        src = jax.random.randint(jax.random.fold_in(_gk, 2), (400000,), 0, 12500, jnp.int32)
        dst = jnp.minimum((12500 * jax.random.uniform(jax.random.fold_in(_gk, 3), (400000,)) ** 2.0).astype(jnp.int32), 99999)
        _o = jnp.argsort(dst, stable=True)
        src = src[_o]
        dst = dst[_o]
        edge_attr_8 = 0.000714719 + 1.00021 * jax.random.normal(jax.random.fold_in(_gk, 11), (400000, 8), jnp.float32)
        return (x, src, dst, edge_attr_8)
    x, src, dst, edge_attr_8 = _rec_inputs()

    def _L0_gnn_setup():
        import jax, jax.numpy as jnp
        import numpy as np
        N_NODES = 6250
        N_EDGES = 50000
        D = 16
        E_FEAT = 8
        N_LAYERS = 3
        BN_EPS = 1e-05

        def _nnconv(x, src, dst, edge_attr, ew, eb, rw, rb):
            W = (edge_attr @ ew + eb).reshape(edge_attr.shape[0], x.shape[1], rw.shape[1])
            xj = x[src]
            msg = jnp.einsum('ei,eio->eo', xj, W)
            agg = jax.ops.segment_sum(msg, dst, num_segments=x.shape[0])
            return agg + x @ rw + rb

        def _batchnorm(x, gamma, beta):
            mean = jnp.mean(x, axis=0)
            var = jnp.mean(jnp.square(x - mean), axis=0)
            return (x - mean) * jax.lax.rsqrt(var + BN_EPS) * gamma + beta
        key = jax.random.key(seed)
        ks = jax.random.split(key, 12)
        x = jax.random.normal(ks[0], (N_NODES, D), dtype=jnp.float32)
        edge_index = jax.random.randint(ks[1], (2, N_EDGES), 0, N_NODES, dtype=jnp.int64)
        edge_attr = jax.random.normal(ks[2], (N_EDGES, E_FEAT), dtype=jnp.float32)
        s = 0.1
        edge_w = jax.random.normal(ks[3], (N_LAYERS, E_FEAT, D * D), dtype=jnp.float32) * s
        edge_b = jax.random.normal(ks[4], (N_LAYERS, D * D), dtype=jnp.float32) * s
        root_w = jax.random.normal(ks[5], (N_LAYERS, D, D), dtype=jnp.float32) * s
        root_b = jax.random.normal(ks[6], (N_LAYERS, D), dtype=jnp.float32) * s
        bn_gamma = jnp.ones((N_LAYERS - 1, D), dtype=jnp.float32)
        bn_beta = jnp.zeros((N_LAYERS - 1, D), dtype=jnp.float32)
        pred_w = jax.random.normal(ks[7], (D, D), dtype=jnp.float32) * s
        pred_b = jax.random.normal(ks[8], (D,), dtype=jnp.float32) * s
        return {'x': x, 'edge_index': edge_index, 'edge_attr': edge_attr, 'edge_w': edge_w, 'edge_b': edge_b, 'root_w': root_w, 'root_b': root_b, 'bn_gamma': bn_gamma, 'bn_beta': bn_beta, 'pred_w': pred_w, 'pred_b': pred_b}
    _L0_gnn_all = _L0_gnn_setup()
    _L0_gnn_in = {k: v for k, v in _L0_gnn_all.items() if k in ('edge_w', 'edge_b', 'root_w', 'root_b', 'bn_gamma', 'bn_beta', 'pred_w', 'pred_b')}
    del _L0_gnn_all
    return {'x': x, 'src': src, 'dst': dst, 'edge_attr_8': edge_attr_8, 'L0_gnn_edge_w': _L0_gnn_in['edge_w'], 'L0_gnn_edge_b': _L0_gnn_in['edge_b'], 'L0_gnn_root_w': _L0_gnn_in['root_w'], 'L0_gnn_root_b': _L0_gnn_in['root_b'], 'L0_gnn_bn_gamma': _L0_gnn_in['bn_gamma'], 'L0_gnn_bn_beta': _L0_gnn_in['bn_beta'], 'L0_gnn_pred_w': _L0_gnn_in['pred_w'], 'L0_gnn_pred_b': _L0_gnn_in['pred_b']}

def reference(x, src, dst, edge_attr_8, L0_gnn_edge_w, L0_gnn_edge_b, L0_gnn_root_w, L0_gnn_root_b, L0_gnn_bn_gamma, L0_gnn_bn_beta, L0_gnn_pred_w, L0_gnn_pred_b):
    import jax
    import jax.numpy as jnp

    def _L0_gnn_ref(x, edge_index, edge_attr, edge_w, edge_b, root_w, root_b, bn_gamma, bn_beta, pred_w, pred_b):
        import jax, jax.numpy as jnp
        import numpy as np
        N_NODES = 6250
        N_EDGES = 50000
        D = 16
        E_FEAT = 8
        N_LAYERS = 3
        BN_EPS = 1e-05

        def _nnconv(x, src, dst, edge_attr, ew, eb, rw, rb):
            W = (edge_attr @ ew + eb).reshape(edge_attr.shape[0], x.shape[1], rw.shape[1])
            xj = x[src]
            msg = jnp.einsum('ei,eio->eo', xj, W)
            agg = jax.ops.segment_sum(msg, dst, num_segments=x.shape[0])
            return agg + x @ rw + rb

        def _batchnorm(x, gamma, beta):
            mean = jnp.mean(x, axis=0)
            var = jnp.mean(jnp.square(x - mean), axis=0)
            return (x - mean) * jax.lax.rsqrt(var + BN_EPS) * gamma + beta
        src, dst = (edge_index[0], edge_index[1])
        h = x
        for i in range(N_LAYERS - 1):
            h = _nnconv(h, src, dst, edge_attr, edge_w[i], edge_b[i], root_w[i], root_b[i])
            h = _batchnorm(h, bn_gamma[i], bn_beta[i])
            h = jax.nn.relu(h)
        h = _nnconv(h, src, dst, edge_attr, edge_w[-1], edge_b[-1], root_w[-1], root_b[-1])
        h = jax.nn.relu(h)
        return h @ pred_w + pred_b
    edge_index = jnp.stack([src, dst])
    h = jnp.maximum(_layernorm(x, axis=-1), 0.0)
    x = x + _L0_gnn_ref(h, edge_index, edge_attr_8, L0_gnn_edge_w, L0_gnn_edge_b, L0_gnn_root_w, L0_gnn_root_b, L0_gnn_bn_gamma, L0_gnn_bn_beta, L0_gnn_pred_w, L0_gnn_pred_b)
    return x

_drawn_inputs = setup_inputs


def setup_inputs(seed=0):
    import zlib

    import numpy as np

    out = dict(_drawn_inputs(seed))
    spreads = {'L0_gnn_bn_gamma': (1.0, 0.2), 'L0_gnn_bn_beta': (0.0, 0.1)}
    factors = {'L0_gnn_root_b': 8.0}
    for name, (base, spread) in spreads.items():
        noise = np.random.default_rng([zlib.crc32(name.encode()), seed]).standard_normal(out[name].shape)
        drawn = base * np.exp(spread * noise) if base else spread * noise
        out[name] = jnp.asarray(drawn.astype(out[name].dtype))
    for name, factor in factors.items():
        out[name] = (out[name] * factor).astype(out[name].dtype)
    return out
```

```python
import concourse.bass as bass
from concourse import mybir

F32 = mybir.dt.float32
I32 = mybir.dt.int32
ALU = mybir.AluOpType
ACT = mybir.ActivationFunctionType
AX = mybir.AxisListType
DVE = mybir.EngineType.DVE
ENGINES = (mybir.EngineType.Pool, mybir.EngineType.Activation, mybir.EngineType.PE,
           mybir.EngineType.DVE, mybir.EngineType.SP)

P = 128
TILES = 5
SLOTS = 5
WINDOW = 64
WIDE = 512
LN_EPS = 1e-5
BN_EPS = 1e-5


def gnn(nc, x, src, dst, edge_attr, edge_w, edge_b, root_w, root_bt, gamma_t, beta_t, pred_w,
        pred_b, out):
    N, D = x.shape
    CHUNKS = src.shape[0]
    FEAT = edge_attr.shape[2] // TILES
    FD = FEAT * D
    LAYERS = edge_w.shape[0]
    ROWS = 125
    COLS = N // ROWS
    BLOCK = CHUNKS // SLOTS
    ROUNDS = CHUNKS // SLOTS
    NB = 500
    NBLOCKS = N // NB
    PER_T = NB // ROWS
    PER_R = COLS // 4
    FURTHER = -(-(N - WINDOW) // WIDE)
    assert ROWS * COLS == N and NBLOCKS * NB == N and BLOCK <= P and CHUNKS % SLOTS == 0
    assert FD == P and src.shape[1:] == (P, TILES)

    h_table = nc.dram_tensor("h_table", (N, D), F32, kind="Internal").ap()

    from contextlib import ExitStack
    ctx = ExitStack()
    with ctx:
        def sb(name, shape, dt=F32):
            return ctx.enter_context(nc.sbuf_tensor(name, shape, dt))

        def sem(name):
            return ctx.enter_context(nc.semaphore(name))

        w_feat = sb("w_feat", [FD, LAYERS, D])
        w_bias = sb("w_bias", [D, LAYERS, D])
        w_root = sb("w_root", [D, LAYERS, D])
        b_root = sb("b_root", [D, LAYERS])
        gamma = sb("gamma", [D, LAYERS - 1])
        beta = sb("beta", [D, LAYERS - 1])
        w_pred = sb("w_pred", [D, D])
        b_pred = sb("b_pred", [ROWS, D])
        ident = sb("ident", [P, P])
        ones = sb("ones", [P, P])
        iota_i = sb("iota_i", [P, WIDE], I32)
        iota = sb("iota", [P, WIDE])
        iota_w = sb("iota_w", [P, WIDE])
        x_rows = sb("x_rows", [ROWS, COLS, D])
        h_rows = sb("h_rows", [ROWS, COLS, D])
        nodes = sb("nodes", [D, N + WIDE])
        ln_a = sb("ln_a", [ROWS, COLS])
        ln_b = sb("ln_b", [ROWS, COLS])
        bn_parts = sb("bn_parts", [D, NBLOCKS, 6])
        bn_mv = sb("bn_mv", [D, 2])
        bn_s = sb("bn_s", [D, 4])
        ln_sq = sb("ln_sq", [ROWS, COLS, D])
        dst_i = sb("dst_i", [P, CHUNKS, TILES], I32)
        dst_rel = sb("dst_rel", [P, CHUNKS, TILES])
        chunk_ends = sb("chunk_ends", [P, 2, CHUNKS])
        ends_col = sb("ends_col", [BLOCK, 2, SLOTS])
        ends_diag = sb("ends_diag", [BLOCK, 2, SLOTS, BLOCK])
        ends_row = sb("ends_row", [P, 2, CHUNKS])
        base_i = sb("base_i", [1, CHUNKS], I32)
        span = sb("span", [1, CHUNKS])
        span_max = sb("span_max", [1, 1])
        further = sb("further", [1, FURTHER])
        further_n = sb("further_n", [1, 1])
        further_i = sb("further_i", [1, 1], I32)
        src_s = [sb(f"src_s{j}", [P, TILES], I32) for j in range(SLOTS)]
        attr_s = [sb(f"attr_s{j}", [P, TILES, FEAT]) for j in range(SLOTS)]
        h_src = [sb(f"h_src{j}", [P, TILES, D]) for j in range(SLOTS)]
        prod = [sb(f"prod{j}", [P, TILES, FEAT, D]) for j in range(SLOTS)]
        onehot = [sb(f"onehot{j}", [P, TILES, WINDOW]) for j in range(SLOTS)]
        g_feat = [sb(f"g_feat{j}", [FD, WINDOW]) for j in range(SLOTS)]
        g_bias = [sb(f"g_bias{j}", [D, WINDOW]) for j in range(SLOTS)]
        wide_hot = sb("wide_hot", [P, TILES, WIDE])
        wide_feat = sb("wide_feat", [FD, WIDE])
        wide_bias = sb("wide_bias", [D, WIDE])

        BANK = [0, 1, 2, 0, 1]
        ps_g = ctx.enter_context(nc.psum_tensor("ps_g", [P, 3, 512], F32))
        ps_a = ctx.enter_context(nc.psum_tensor("ps_a", [P, 3, 512], F32))
        ps_n = ctx.enter_context(nc.psum_tensor("ps_n", [P, 2, 512], F32))

        s_weights = sem("s_weights")
        s_x = sem("s_x")
        s_dst = sem("s_dst")
        s_const = sem("s_const")
        s_iota = sem("s_iota")
        s_ln = sem("s_ln")
        s_ln_std = sem("s_ln_std")
        s_prep = sem("s_prep")
        s_ends_t = sem("s_ends_t")
        s_ends_b = sem("s_ends_b")
        s_bases = sem("s_bases")
        s_table = sem("s_table")
        s_rows = sem("s_rows")
        s_turn = sem("s_turn")
        s_turned = sem("s_turned")
        s_src = [sem(f"s_src{j}") for j in range(SLOTS)]
        s_attr = [sem(f"s_attr{j}") for j in range(SLOTS)]
        s_gath = [sem(f"s_gath{j}") for j in range(SLOTS)]
        s_form = sem("s_form")
        s_g = sem("s_g")
        s_gcopy = sem("s_gcopy")
        s_agg = sem("s_agg")
        s_add = sem("s_add")
        s_bn = sem("s_bn")
        s_bn_std = sem("s_bn_std")
        s_bn_done = sem("s_bn_done")
        s_relu = sem("s_relu")
        s_out = sem("s_out")
        s_fin = sem("s_fin")
        w_src, w_attr, w_gath, w_rows = sem("w_src"), sem("w_attr"), sem("w_gath"), sem("w_rows")
        w_go_sp, w_form, w_g, w_copy, w_agg = (sem("w_go_sp"), sem("w_form"), sem("w_g"),
                                                sem("w_copy"), sem("w_agg"))
        w_go_pool, w_iota, w_prod, w_add = sem("w_go_pool"), sem("w_iota"), sem("w_prod"), sem("w_add")
        s_start = sem("s_start")
        s_whole = sem("s_whole")

        rows_of = lambda t: t.rearrange("(p j) d -> p j d", j=COLS)
        by_col = nodes[:, 0:N].rearrange("q (p j) -> q j p", j=COLS)
        by_row = nodes[:, 0:N].rearrange("q (p j) -> q p j", j=COLS)

        TURNS_IN = COLS // PER_T
        TURNS_OUT = COLS // PER_R

        def turns_before(layer):
            return TURNS_IN + layer * (NBLOCKS + TURNS_OUT)

        def further_windows(eng, engine_type, body):
            n = nc.values_load(further_i[0:1, 0:1], engines=(engine_type,), min_val=0,
                               max_val=FURTHER,
                               skip_runtime_bounds_check_because="a sum of FURTHER zeros or ones")
            with eng.If(n > 0):
                with eng.Fori(0, n) as w:
                    body.window(w)
                    with eng.Fori(0, CHUNKS) as c:
                        body.chunk(w, c)
            with eng.Else():
                eng.nop()

        class Body:
            def __init__(self, window, chunk):
                self.window, self.chunk = window, chunk

        def taken(eng, s, n):
            eng.wait_ge(s, n)
            eng.sem_clear(s)

        def ends_bank(m, k):
            n = m * SLOTS + k
            return (ps_g if n < 6 else ps_a)[:, n // 2 % 3, n % 2 * P:(n % 2 + 1) * P]

        block = ctx.enter_context(nc.Block())

        @block.sync
        def _(sp):
            sp.dma_start(x_rows[:], rows_of(x)).then_inc(s_x, 16)
            for j in range(SLOTS):
                sp.dma_start(src_s[j][:], src[j]).then_inc(s_src[j], 16)
                sp.dma_start(attr_s[j][:], edge_attr[j].rearrange("p (t f) -> p t f", t=TILES)) \
                  .then_inc(s_attr[j], 16)
            sp.dma_start(dst_i[:], dst).then_inc(s_dst, 16)
            for tile, view in (
                (w_feat[:], edge_w.rearrange("l f (i o) -> (f i) l o", o=D)),
                (w_bias[:], edge_b.rearrange("l (i o) -> i l o", o=D)),
                (w_root[:], root_w.rearrange("l i o -> i l o")),
                (b_root[:], root_bt), (gamma[:], gamma_t), (beta[:], beta_t),
                (w_pred[:], pred_w), (b_pred[:], pred_b.to_broadcast([ROWS, D])),
            ):
                sp.dma_start(tile, view).then_inc(s_weights, 16)

            for layer in range(LAYERS):
                done = layer * CHUNKS
                sp.wait_ge(s_rows, layer + 1 if layer == 0 else 1 + layer * TURNS_OUT)
                sp.dma_start(rows_of(h_table), h_rows[:]).then_inc(s_table, 16)

                def refill(c, j):
                    sp.wait_ge(s_g, c - SLOTS + 1 + done)
                    sp.dma_start(src_s[j][:], src[bass.ds(c, 1)].rearrange("a p t -> (a p) t")) \
                      .then_inc(s_src[j], 16)
                    sp.dma_start(attr_s[j][:], edge_attr[bass.ds(c, 1)].rearrange("a p (t f) -> (a p) t f", t=TILES)) \
                      .then_inc(s_attr[j], 16)

                with sp.Fori(1, ROUNDS) as r:
                    for j in range(SLOTS):
                        refill(r * SLOTS + j, j)

                def window(w):
                    pass

                def chunk(w, c):
                    taken(sp, w_go_sp, 1)
                    sp.dma_start(src_s[0][:], src[bass.ds(c, 1)].rearrange("a p t -> (a p) t")).then_inc(w_src, 16)
                    sp.dma_start(attr_s[0][:], edge_attr[bass.ds(c, 1)].rearrange("a p (t f) -> (a p) t f", t=TILES)).then_inc(w_attr, 16)

                sp.wait_ge(s_bases, 1)
                sp.wait_ge(s_form, (done + CHUNKS) * 2)
                further_windows(sp, mybir.EngineType.SP, Body(window, chunk))
                if layer < LAYERS - 1:
                    sp.wait_ge(s_whole, layer + 1)
                    for j in range(SLOTS):
                        sp.dma_start(src_s[j][:], src[j]).then_inc(s_src[j], 16)
                        sp.dma_start(attr_s[j][:], edge_attr[j].rearrange("p (t f) -> p t f", t=TILES)) \
                          .then_inc(s_attr[j], 16)

            sp.wait_ge(s_fin, 2 * TURNS_OUT)
            sp.dma_start(rows_of(out), h_rows[:]).then_inc(s_out, 16)
            sp.wait_ge(s_out, 16)

        @block.gpsimd
        def _(pool):
            pool.memset(ident[:], 0.0).then_inc(s_const, 1)
            pool.memset(ones[:], 1.0).then_inc(s_const, 1)
            pool.iota(iota_i[:], pattern=[[1, WIDE]], base=0, channel_multiplier=0).then_inc(s_const, 1)
            pool.wait_ge(s_const, 3)
            pool.affine_select(out=ident[:], in_=ident[:], compare_op=ALU.not_equal, fill=1.0,
                               base=0, pattern=[[-1, P]], channel_multiplier=1).then_inc(s_const, 1)

            def gather(j, signal):
                for t in range(TILES):
                    pool.indirect_dma_start(
                        out=h_src[j][:, t, :], out_offset=None, in_=h_table,
                        in_offset=bass.IndirectOffsetOnAxis(ap=src_s[j][:, t:t + 1], axis=0)
                    ).then_inc(signal, 16)

            for layer in range(LAYERS):
                done = layer * CHUNKS
                pool.wait_ge(s_table, 16 * (layer + 1))

                def step(r, j, first):
                    c = r * SLOTS + j
                    pool.wait_ge(s_src[j], (r + 1 + layer * ROUNDS) * 16)
                    pool.sem_inc(s_start, 1)
                    gather(j, s_gath[j])

                for j in range(SLOTS):
                    step(0, j, True)
                with pool.Fori(1, ROUNDS) as r:
                    for j in range(SLOTS):
                        step(r, j, False)

                def chunk(w, c):
                    taken(pool, w_go_pool, 1)
                    taken(pool, w_src, 16)
                    gather(0, w_gath)
                    pool.wait_ge(w_gath, 16 * TILES)
                    pool.dma_reset(range(w_gath.num, w_gath.num + 1))
                    pool.sem_clear(w_gath)
                    pool.sem_inc(w_rows, 1)

                pool.wait_ge(s_bases, 1)
                pool.wait_ge(s_g, done + CHUNKS)
                further_windows(pool, mybir.EngineType.Pool, Body(lambda w: None, chunk))

        @block.tensor
        def _(pe):
            mm = nc.tensor.matmul
            pe.wait_ge(s_const, 4)
            pe.wait_ge(s_rows, 1)
            for k in range(TURNS_IN):
                if k >= 2:
                    pe.wait_ge(s_turned, k - 1)
                for q in range(PER_T):
                    last = nc.tensor.transpose(ps_n[0:D, k % 2, q * ROWS:(q + 1) * ROWS],
                                               h_rows[:, k * PER_T + q, :], ident[0:ROWS, 0:ROWS])
                last.then_inc(s_turn, 1)
            pe.wait_ge(s_prep, 3)
            for k in range(SLOTS):
                for m in range(2):
                    last = nc.tensor.transpose(ends_bank(m, k)[0:BLOCK, :],
                                               chunk_ends[:, m, k * BLOCK:(k + 1) * BLOCK], ident[:])
            last.then_inc(s_ends_t, 1)
            pe.wait_ge(s_prep, 6)
            for k in range(SLOTS):
                for m in range(2):
                    last = mm(ends_bank(m, k)[:, 0:BLOCK], ones[0:BLOCK, :],
                              ends_diag[:, m, k, :], start=True, stop=True)
            last.then_inc(s_ends_b, 1)
            pe.wait_ge(s_weights, 8 * 16)

            def reduce_chunk(feat, bias, h, z, hot):
                for t in range(TILES):
                    mm(feat, z[:, t, :, :].rearrange("p f i -> p (f i)"), hot[:, t, :],
                       start=(t == 0), stop=(t == TILES - 1))
                for t in range(TILES):
                    last = mm(bias, h[:, t, :], hot[:, t, :], start=(t == 0), stop=(t == TILES - 1))
                return last

            def apply_w(layer, to, feat, bias):
                mm(to, w_feat[:, layer, :], feat, start=True, stop=False)
                return mm(to, w_bias[:, layer, :], bias, start=False, stop=True)

            for layer in range(LAYERS):
                done = layer * CHUNKS
                before = turns_before(layer)
                for b in range(NBLOCKS):
                    n = before + b
                    pe.wait_ge(s_turned, n if layer == 0 and b == 0 else n - 1)
                    mm(ps_n[0:D, n % 2, 0:NB], w_root[:, layer, :], nodes[:, b * NB:(b + 1) * NB],
                       start=True, stop=True).then_inc(s_turn, 1)
                if layer == 0:
                    pe.wait_ge(s_bases, 1)

                def reduce_step(r, j, first):
                    c = r * SLOTS + j
                    pe.wait_ge(s_form, (c + 1 + done) * 2)
                    if not (first and layer == 0 and j < 2):
                        pe.wait_ge(s_gcopy, (c - 1 + done) * 2)
                    reduce_chunk(ps_g[:, BANK[j], 0:WINDOW], ps_g[0:D, BANK[j], WINDOW:2 * WINDOW],
                                 h_src[j], prod[j], onehot[j]).then_inc(s_g, 1)

                def apply_step(r, j, first):
                    c = r * SLOTS + j
                    pe.wait_ge(s_gcopy, (c + 1 + done) * 2)
                    if not (first and layer == 0 and j < 2):
                        pe.wait_ge(s_add, c - 1 + done)
                    apply_w(layer, ps_a[0:D, BANK[j], 0:WINDOW], g_feat[j][:],
                            g_bias[j][:]).then_inc(s_agg, 1)

                for j in range(SLOTS):
                    reduce_step(0, j, True)
                    if j:
                        apply_step(0, j - 1, True)
                with pe.Fori(1, ROUNDS) as r:
                    for j in range(SLOTS):
                        reduce_step(r, j, False)
                        if j:
                            apply_step(r, j - 1, False)
                        else:
                            apply_step(r - 1, SLOTS - 1, False)
                apply_step(ROUNDS - 1, SLOTS - 1, False)

                def chunk(w, c):
                    taken(pe, w_form, 2)
                    reduce_chunk(ps_g[:, 0, :], ps_g[0:D, 1, :], h_src[0], prod[0], wide_hot).then_inc(w_g, 1)
                    taken(pe, w_copy, 2)
                    apply_w(layer, ps_a[0:D, 0, :], wide_feat[:], wide_bias[:]).then_inc(w_agg, 1)

                pe.wait_ge(s_gcopy, 2 * (done + CHUNKS))
                pe.wait_ge(s_add, done + CHUNKS)
                further_windows(pe, mybir.EngineType.PE, Body(lambda w: None, chunk))

                if layer < LAYERS - 1:
                    for k in range(TURNS_OUT):
                        n = before + NBLOCKS + k
                        pe.wait_ge(s_relu, layer * TURNS_OUT + k + 1)
                        pe.wait_ge(s_turned, n - 1)
                        for q in range(PER_R):
                            last = nc.tensor.transpose(ps_n[0:ROWS, n % 2, q * D:(q + 1) * D],
                                                       by_col[:, k * PER_R + q, :], ident[0:D, 0:D])
                        last.then_inc(s_turn, 1)
                else:
                    for k in range(TURNS_OUT):
                        n = before + NBLOCKS + k
                        pe.wait_ge(s_relu, layer * TURNS_OUT + k + 1)
                        if k >= 2:
                            pe.wait_ge(s_fin, 2 * (k - 1))
                        else:
                            pe.wait_ge(s_turned, n - k)
                        for q in range(PER_R):
                            last = mm(ps_n[0:ROWS, n % 2, q * D:(q + 1) * D],
                                      by_col[:, k * PER_R + q, :], w_pred[:], start=True, stop=True)
                        last.then_inc(s_turn, 1)

        @block.scalar
        def _(act):
            copy = lambda o, i: nc.scalar.activation(o, i, ACT.Copy)
            act.wait_ge(s_ln, 6)
            nc.scalar.activation(ln_b[:], ln_a[:], ACT.Sqrt).then_inc(s_ln_std, 1)
            for k in range(TURNS_IN):
                act.wait_ge(s_turn, k + 1)
                copy(by_col[:, k * PER_T:(k + 1) * PER_T, :],
                     ps_n[0:D, k % 2, 0:NB].rearrange("q (j p) -> q j p", p=ROWS)).then_inc(s_turned, 1)
            act.wait_ge(s_weights, 8 * 16)

            for layer in range(LAYERS):
                done = layer * CHUNKS
                before = turns_before(layer)
                for b in range(NBLOCKS):
                    n = before + b
                    act.wait_ge(s_turn, n + 1)
                    nc.scalar.activation(nodes[:, b * NB:(b + 1) * NB], ps_n[0:D, n % 2, 0:NB],
                                         ACT.Identity, bias=b_root[:, layer:layer + 1]).then_inc(s_turned, 1)

                def step(r, j, first):
                    c = r * SLOTS + j
                    act.wait_ge(s_g, c + 1 + done)
                    if not (first and layer == 0):
                        act.wait_ge(s_agg, c - SLOTS + 1 + done)
                    copy(g_feat[j][:], ps_g[:, BANK[j], 0:WINDOW]).then_inc(s_gcopy, 1)
                    copy(g_bias[j][:], ps_g[0:D, BANK[j], WINDOW:2 * WINDOW]).then_inc(s_gcopy, 1)

                for j in range(SLOTS):
                    step(0, j, True)
                with act.Fori(1, ROUNDS) as r:
                    for j in range(SLOTS):
                        step(r, j, False)

                def chunk(w, c):
                    taken(act, w_g, 1)
                    copy(wide_feat[:], ps_g[:, 0, :]).then_inc(w_copy, 1)
                    copy(wide_bias[:], ps_g[0:D, 1, :]).then_inc(w_copy, 1)

                act.wait_ge(s_bases, 1)
                further_windows(act, mybir.EngineType.Activation, Body(lambda w: None, chunk))

                if layer < LAYERS - 1:
                    act.wait_ge(s_bn, (layer + 1) * (NBLOCKS + 2))
                    nc.scalar.activation(bn_s[:, 1:2], bn_s[:, 0:1], ACT.Sqrt).then_inc(s_bn_std, 1)
                    act.wait_ge(s_bn_done, 4 * (layer + 1))
                else:
                    act.wait_ge(s_whole, LAYERS)
                scale = bn_s[:, 2:3] if layer < LAYERS - 1 else 1.0
                shift = bn_s[:, 3:4] if layer < LAYERS - 1 else 0.0

                def relu(k):
                    part = by_row[:, :, k * PER_R:(k + 1) * PER_R]
                    nc.scalar.activation(part, part, ACT.Relu, bias=shift, scale=scale).then_inc(s_relu, 1)

                relu(0)
                for k in range(TURNS_OUT):
                    if k + 1 < TURNS_OUT:
                        relu(k + 1)
                    if layer < LAYERS - 1:
                        n = before + NBLOCKS + k
                        act.wait_ge(s_turn, n + 1)
                        if k == 0:
                            act.wait_ge(s_table, 16 * (layer + 1))
                        copy(h_rows[:, k * PER_R:(k + 1) * PER_R, :].rearrange("p j d -> p (j d)"),
                             ps_n[0:ROWS, n % 2, 0:PER_R * D]).then_inc(s_turned, 1)
                        act.wait_ge(s_turned, n + 1)
                        act.sem_inc(s_rows, 1)

        @block.vector
        def _(dve):
            v = nc.vector
            dve.wait_ge(s_x, 16)
            wide = lambda t: t[:].unsqueeze(2).to_broadcast([ROWS, COLS, D])
            v.tensor_reduce(ln_a[:], x_rows[:], AX.X, ALU.add).then_inc(s_ln, 1)
            dve.wait_ge(s_ln, 1)
            v.tensor_scalar(ln_b[:], ln_a[:], 1.0 / D, None, ALU.mult).then_inc(s_ln, 1)
            dve.wait_ge(s_ln, 2)
            v.tensor_tensor(h_rows[:], x_rows[:], wide(ln_b), ALU.subtract).then_inc(s_ln, 1)
            dve.wait_ge(s_ln, 3)
            squares = ln_sq[:]
            v.tensor_tensor(squares, h_rows[:], h_rows[:], ALU.mult).then_inc(s_ln, 1)
            dve.wait_ge(s_ln, 4)
            v.tensor_reduce(ln_b[:], squares, AX.X, ALU.add).then_inc(s_ln, 1)
            dve.wait_ge(s_ln, 5)
            v.tensor_scalar(ln_a[:], ln_b[:], 1.0 / D, LN_EPS, ALU.mult, ALU.add).then_inc(s_ln, 1)
            dve.wait_ge(s_ln_std, 1)
            v.reciprocal(ln_a[:], ln_b[:]).then_inc(s_ln, 1)
            dve.wait_ge(s_ln, 7)
            v.tensor_tensor(h_rows[:], h_rows[:], wide(ln_a), ALU.mult).then_inc(s_ln, 1)
            dve.wait_ge(s_ln, 8)
            v.tensor_scalar(h_rows[:], h_rows[:], 0.0, None, ALU.max).then_inc(s_rows, 1)

            dve.wait_ge(s_const, 4)
            v.tensor_copy(iota[:], iota_i[:]).then_inc(s_iota, 1)
            v.memset(nodes[:, N:N + WIDE], 0.0)
            dve.wait_ge(s_dst, 16)
            v.tensor_copy(dst_rel[:], dst_i[:]).then_inc(s_prep, 1)
            dve.wait_ge(s_prep, 1)
            v.tensor_reduce(chunk_ends[:, 0, :], dst_rel[:], AX.X, ALU.min).then_inc(s_prep, 1)
            v.tensor_reduce(chunk_ends[:, 1, :], dst_rel[:], AX.X, ALU.max).then_inc(s_prep, 1)
            dve.wait_ge(s_ends_t, 1)
            for m, op in enumerate((ALU.min, ALU.max)):
                for k in range(SLOTS):
                    last = v.tensor_reduce(ends_col[:, m, k:k + 1], ends_bank(m, k)[0:BLOCK, :], AX.X, op)
                last.then_inc(s_prep, 1)
            dve.wait_ge(s_prep, 5)
            v.tensor_tensor(
                ends_diag[:].rearrange("p m k c -> p (m k) c"),
                ends_col[:].rearrange("p m k -> p (m k)").unsqueeze(2).to_broadcast([BLOCK, 2 * SLOTS, BLOCK]),
                ident[0:BLOCK, 0:BLOCK].unsqueeze(1).to_broadcast([BLOCK, 2 * SLOTS, BLOCK]),
                ALU.mult).then_inc(s_prep, 1)
            dve.wait_ge(s_ends_b, 1)
            for m in range(2):
                for k in range(SLOTS):
                    last = v.tensor_copy(ends_row[:, m, k * BLOCK:(k + 1) * BLOCK], ends_bank(m, k)[:, 0:BLOCK])
                last.then_inc(s_prep, 1)
            dve.wait_ge(s_prep, 8)
            v.tensor_tensor(dst_rel[:], dst_rel[:], ends_row[:, 0, :].unsqueeze(2).to_broadcast([P, CHUNKS, TILES]),
                            ALU.subtract).then_inc(s_prep, 1)
            v.tensor_copy(base_i[:], ends_row[0:1, 0, :]).then_inc(s_prep, 1)
            v.tensor_tensor(span[:], ends_row[0:1, 1, :], ends_row[0:1, 0, :], ALU.subtract).then_inc(s_prep, 1)
            dve.wait_ge(s_prep, 11)
            dve.wait_ge(s_iota, 1)
            v.tensor_reduce(span_max[:], span[:], AX.X, ALU.max).then_inc(s_prep, 1)
            v.tensor_scalar(further[:], iota[0:1, 0:FURTHER], float(WIDE), float(WINDOW), ALU.mult, ALU.add) \
                .then_inc(s_prep, 1)
            dve.wait_ge(s_prep, 13)
            v.tensor_scalar(further[:], further[:], span_max[:], None, ALU.is_le).then_inc(s_prep, 1)
            dve.wait_ge(s_prep, 14)
            v.tensor_reduce(further_n[:], further[:], AX.X, ALU.add).then_inc(s_prep, 1)
            dve.wait_ge(s_prep, 15)
            v.tensor_copy(further_i[:], further_n[:]).then_inc(s_bases, 1)
            dve.wait_ge(s_bases, 1)

            def products(j):
                return v.tensor_tensor(
                    prod[j][:],
                    attr_s[j][:].unsqueeze(3).to_broadcast([P, TILES, FEAT, D]),
                    h_src[j][:].unsqueeze(2).to_broadcast([P, TILES, FEAT, D]), ALU.mult)

            def one_hots(hot, c, row, width):
                return v.tensor_tensor(
                    hot[:], dst_rel[:, bass.ds(c, 1), :].rearrange("p a t -> p (a t)").unsqueeze(2).to_broadcast([P, TILES, width]),
                    row.unsqueeze(1).to_broadcast([P, TILES, width]), ALU.is_equal)

            for layer in range(LAYERS):
                done = layer * CHUNKS

                def form_step(r, j, first):
                    c = r * SLOTS + j
                    if not (first and layer == 0):
                        dve.wait_ge(s_g, c - SLOTS + 1 + done)
                    one_hots(onehot[j], c, iota[:, 0:WINDOW], WINDOW).then_inc(s_form, 1)
                    dve.wait_ge(s_attr[j], (r + 1 + layer * ROUNDS) * 16)
                    dve.wait_ge(s_gath[j], (r + 1 + layer * ROUNDS) * 16 * TILES)
                    products(j).then_inc(s_form, 1)

                def add_step(r, j, first, base):
                    c = r * SLOTS + j
                    dve.wait_ge(s_agg, c + 1 + done)
                    if not (first and layer == 0 and j == 0):
                        dve.wait_ge(s_add, c + done)
                    at = nodes[:, bass.ds(base, WINDOW)]
                    v.tensor_tensor(at, at, ps_a[0:D, BANK[j], 0:WINDOW], ALU.add).then_inc(s_add, 1)

                def base_of(c):
                    return nc.values_load(base_i[0:1, bass.ds(c, 1)], engines=(DVE,), min_val=0,
                                          max_val=N, skip_runtime_bounds_check_because="a node's number")

                for j in range(SLOTS):
                    form_step(0, j, True)
                    if j == 0:
                        dve.wait_ge(s_turned, turns_before(layer) + NBLOCKS)
                    if j >= 2:
                        add_step(0, j - 2, True, base_of(j - 2))
                with dve.Fori(1, ROUNDS) as r:
                    at = [base_of(r * SLOTS + j - 2) for j in range(SLOTS)]
                    for j in range(SLOTS):
                        form_step(r, j, False)
                        if j < 2:
                            add_step(r - 1, j - 2 + SLOTS, False, at[j])
                        else:
                            add_step(r, j - 2, False, at[j])
                for j in (SLOTS - 2, SLOTS - 1):
                    add_step(ROUNDS - 1, j, False, base_of((ROUNDS - 1) * SLOTS + j))
                dve.wait_ge(s_add, done + CHUNKS)

                v.tensor_scalar(iota_w[:], iota[:], float(WINDOW - WIDE), None, ALU.add).then_inc(w_iota, 1)
                dve.sem_inc(w_add, 1)

                def window(w):
                    taken(dve, w_iota, 1)
                    v.tensor_scalar(iota_w[:], iota_w[:], float(WIDE), None, ALU.add).then_inc(w_iota, 1)

                def chunk(w, c):
                    dve.sem_inc(w_go_sp, 1)
                    dve.sem_inc(w_go_pool, 1)
                    dve.wait_ge(w_iota, 1)
                    one_hots(wide_hot, c, iota_w[:], WIDE).then_inc(w_form, 1)
                    taken(dve, w_attr, 16)
                    taken(dve, w_rows, 1)
                    products(0).then_inc(w_form, 1)
                    base = nc.values_load(base_i[0:1, bass.ds(c, 1)], engines=(DVE,), min_val=0,
                                          max_val=N - 1, skip_runtime_bounds_check_because="a node's number")
                    start = dve.snap(base + w * WIDE + WINDOW)
                    clamped = nc.s_assert_within(start - (start - N) * (start > N), 0, N,
                                                 skip_runtime_bounds_check_because="cut off at N")
                    taken(dve, w_agg, 1)
                    at = nodes[:, bass.ds(clamped, WIDE)]
                    taken(dve, w_add, 1)
                    v.tensor_tensor(at, at, ps_a[0:D, 0, :], ALU.add).then_inc(w_add, 1)
                    dve.wait_ge(w_add, 1)

                further_windows(dve, DVE, Body(window, chunk))
                taken(dve, w_iota, 1)
                taken(dve, w_add, 1)
                dve.sem_inc(s_whole, 1)

                if layer < LAYERS - 1:
                    for b in range(NBLOCKS):
                        v.bn_stats(bn_parts[:, b, :], nodes[:, b * NB:(b + 1) * NB]).then_inc(s_bn, 1)
                    before = layer * (NBLOCKS + 2)
                    dve.wait_ge(s_bn, before + NBLOCKS)
                    v.bn_aggr(bn_mv[:], bn_parts[:].rearrange("q b s -> q (b s)")).then_inc(s_bn, 1)
                    dve.wait_ge(s_bn, before + NBLOCKS + 1)
                    v.tensor_scalar(bn_s[:, 0:1], bn_mv[:, 1:2], BN_EPS, None, ALU.add).then_inc(s_bn, 1)
                    dve.wait_ge(s_bn_std, layer + 1)
                    v.reciprocal(bn_s[:, 2:3], bn_s[:, 1:2]).then_inc(s_bn_done, 1)
                    dve.wait_ge(s_bn_done, 4 * layer + 1)
                    v.tensor_tensor(bn_s[:, 2:3], bn_s[:, 2:3], gamma[:, layer:layer + 1], ALU.mult).then_inc(s_bn_done, 1)
                    dve.wait_ge(s_bn_done, 4 * layer + 2)
                    v.tensor_tensor(bn_s[:, 3:4], bn_mv[:, 0:1], bn_s[:, 2:3], ALU.mult).then_inc(s_bn_done, 1)
                    dve.wait_ge(s_bn_done, 4 * layer + 3)
                    v.tensor_tensor(bn_s[:, 3:4], beta[:, layer:layer + 1], bn_s[:, 3:4], ALU.subtract).then_inc(s_bn_done, 1)

            dve.wait_ge(s_table, 16 * LAYERS)
            for k in range(TURNS_OUT):
                n = turns_before(LAYERS - 1) + NBLOCKS + k
                dve.wait_ge(s_turn, n + 1)
                rows = h_rows[:, k * PER_R:(k + 1) * PER_R, :]
                v.tensor_tensor(rows, ps_n[0:ROWS, n % 2, 0:PER_R * D].rearrange("p (j d) -> p j d", d=D),
                                b_pred[:].unsqueeze(1).to_broadcast([ROWS, PER_R, D]), ALU.add).then_inc(s_fin, 1)
                dve.wait_ge(s_fin, 2 * k + 1)
                v.tensor_tensor(rows, rows, x_rows[:, k * PER_R:(k + 1) * PER_R, :], ALU.add).then_inc(s_fin, 1)


def kernel(**inputs):
    import numpy as np
    import concourse.bacc as bacc
    from concourse.bass_utils import run_bass_kernel_spmd

    def edges_by_chunk(a):
        return np.ascontiguousarray(np.asarray(a).reshape(-1, P, TILES * (a.shape[1] if a.ndim > 1 else 1)))

    arrays = {
        "x": inputs["x"],
        "src": edges_by_chunk(inputs["src"]),
        "dst": np.asarray(inputs["dst"]).reshape(-1, P, TILES).transpose(1, 0, 2),
        "edge_attr": edges_by_chunk(inputs["edge_attr_8"]),
        "edge_w": inputs["L0_gnn_edge_w"],
        "edge_b": inputs["L0_gnn_edge_b"],
        "root_w": inputs["L0_gnn_root_w"],
        "root_bt": np.asarray(inputs["L0_gnn_root_b"]).T,
        "gamma_t": np.asarray(inputs["L0_gnn_bn_gamma"]).T,
        "beta_t": np.asarray(inputs["L0_gnn_bn_beta"]).T,
        "pred_w": inputs["L0_gnn_pred_w"],
        "pred_b": np.asarray(inputs["L0_gnn_pred_b"]).reshape(1, -1),
    }
    arrays = {f"in_{k}": np.ascontiguousarray(a) for k, a in arrays.items()}
    nc = bacc.Bacc("TRN2", target_bir_lowering=False, num_devices=1)
    args = [nc.dram_tensor(k, a.shape, mybir.dt.from_np(a.dtype), kind="ExternalInput").ap()
            for k, a in arrays.items()]
    out = nc.dram_tensor("out", inputs["x"].shape, F32, kind="ExternalOutput").ap()
    gnn(nc, *args, out)
    r = run_bass_kernel_spmd(nc, [arrays], core_ids=[0])
    return r.results[0]["out"]
```

```python
import concourse.bass as bass
from concourse import mybir

F32 = mybir.dt.float32
I32 = mybir.dt.int32
F16 = mybir.dt.float16
BF16 = mybir.dt.bfloat16
ALU = mybir.AluOpType
ACT = mybir.ActivationFunctionType
AX = mybir.AxisListType
DVE = mybir.EngineType.DVE
ENGINES = (mybir.EngineType.Pool, mybir.EngineType.Activation, mybir.EngineType.PE,
           mybir.EngineType.DVE, mybir.EngineType.SP)

P = 128
TILES = 5
SLOTS = 5
WINDOW = 64
WIDE = 512
LN_EPS = 1e-5
BN_EPS = 1e-5


PICKS = [1, 1, 1, 1, 1]
PICKED = max(PICKS)
PARTS = 5
SPLITS = 3
ROUND = 1.5 * 2 ** 23


def gnn(nc, x, src, src_rows, src_cols, dst, edge_attr, edge_w, edge_b, root_w, root_bt, gamma_t, beta_t, pred_w,
        pred_b, out):
    N, D = x.shape
    CHUNKS = src.shape[0]
    FEAT = edge_attr.shape[2] // TILES
    FD = FEAT * D
    LAYERS = edge_w.shape[0]
    ROWS = 125
    COLS = N // ROWS
    BLOCK = CHUNKS // SLOTS
    ROUNDS = CHUNKS // SLOTS
    NB = 500
    NBLOCKS = N // NB
    PER_T = NB // ROWS
    PER_R = COLS // 4
    FURTHER = -(-(N - WINDOW) // WIDE)
    assert ROWS * COLS == N and NBLOCKS * NB == N and BLOCK <= P and CHUNKS % SLOTS == 0
    assert FD == P and src.shape[1:] == (P, TILES)

    PART = COLS // PARTS
    ROWN = ROWS * PARTS
    UNITS = sum(PICKS)
    FIRST_UNIT = [sum(PICKS[:j]) for j in range(SLOTS)]
    CROWS = CHUNKS // BLOCK
    assert PARTS * PART == COLS and ROWN <= 2048 and PART * D <= 512

    code_table = nc.dram_tensor("code_table", (CHUNKS, PICKED * P), F16, kind="Internal").ap()
    h_table = nc.dram_tensor("h_table", (N, D), F32, kind="Internal").ap()

    from contextlib import ExitStack
    ctx = ExitStack()
    with ctx:
        def sb(name, shape, dt=F32):
            return ctx.enter_context(nc.sbuf_tensor(name, shape, dt))

        def sem(name):
            return ctx.enter_context(nc.semaphore(name))

        w_feat = sb("w_feat", [FD, LAYERS, D])
        w_bias = sb("w_bias", [D, LAYERS, D])
        w_root = sb("w_root", [D, LAYERS, D])
        b_root = sb("b_root", [D, LAYERS])
        gamma = sb("gamma", [D, LAYERS - 1])
        beta = sb("beta", [D, LAYERS - 1])
        w_pred = sb("w_pred", [D, D])
        b_pred = sb("b_pred", [ROWS, D])
        ident = sb("ident", [P, P])
        ones = sb("ones", [P, P])
        iota_i = sb("iota_i", [P, WIDE], I32)
        iota = sb("iota", [P, WIDE])
        iota_w = sb("iota_w", [P, WIDE])
        x_rows = sb("x_rows", [ROWS, COLS, D])
        h_rows = sb("h_rows", [ROWS, COLS, D])
        nodes = sb("nodes", [D, N + WIDE])
        ln_a = sb("ln_a", [ROWS, COLS])
        ln_b = sb("ln_b", [ROWS, COLS])
        bn_parts = sb("bn_parts", [D, NBLOCKS, 6])
        bn_mv = sb("bn_mv", [D, 2])
        bn_s = sb("bn_s", [D, 4])
        ln_sq = sb("ln_sq", [ROWS, COLS, D])
        dst_i = sb("dst_i", [P, CHUNKS, TILES], I32)
        dst_rel = sb("dst_rel", [P, CHUNKS, TILES])
        chunk_ends = sb("chunk_ends", [P, 2, CHUNKS])
        ends_col = sb("ends_col", [BLOCK, 2, SLOTS])
        ends_diag = sb("ends_diag", [BLOCK, 2, SLOTS, BLOCK])
        ends_row = sb("ends_row", [P, 2, CHUNKS])
        base_i = sb("base_i", [1, CHUNKS], I32)
        span = sb("span", [1, CHUNKS])
        span_max = sb("span_max", [1, 1])
        further = sb("further", [1, FURTHER])
        further_n = sb("further_n", [1, 1])
        further_i = sb("further_i", [1, 1], I32)
        src_s = [sb(f"src_s{j}", [P, TILES], I32) for j in range(SLOTS)]
        attr_s = [sb(f"attr_s{j}", [P, TILES, FEAT]) for j in range(SLOTS)]
        h_src = [sb(f"h_src{j}", [P, TILES, D]) for j in range(SLOTS)]
        prod = [sb(f"prod{j}", [P, TILES, FEAT, D]) for j in range(SLOTS)]
        onehot = [sb(f"onehot{j}", [P, TILES, WINDOW]) for j in range(SLOTS)]
        g_feat = [sb(f"g_feat{j}", [FD, WINDOW]) for j in range(SLOTS)]
        g_bias = [sb(f"g_bias{j}", [D, WINDOW]) for j in range(SLOTS)]
        src_i = sb("src_i", [BLOCK, CROWS, PICKED * P], I32)
        code = sb("code", [BLOCK, CROWS, PICKED * P], F16)
        cols_i = sb("cols_i", [P, CHUNKS, PICKED], I32)
        cols_q = sb("cols_q", [P, CHUNKS, PICKED])
        rest = sb("rest", [P, CHUNKS, PICKED])
        rowpart_i = sb("rowpart_i", [P, PARTS], I32)
        rowpart = sb("rowpart", [P, PARTS], F16)
        h_split = sb("h_split", [ROWS, SPLITS, PARTS, PART * D], BF16)
        h_left = sb("h_left", [ROWS, COLS, D])
        code_s = [sb(f"code_s{j}", [ROWS, PICKED, P], F16) for j in range(SLOTS)]
        pick_hot = [sb(f"pick_hot{j}", [ROWS, PICKED, PARTS, P], BF16) for j in range(SLOTS)]
        picked = [sb(f"picked{k}", [P, D, PART]) for k in range(3)]
        wide_hot = sb("wide_hot", [P, TILES, WIDE])
        wide_feat = sb("wide_feat", [FD, WIDE])
        wide_bias = sb("wide_bias", [D, WIDE])

        ps_g = ctx.enter_context(nc.psum_tensor("ps_g", [P, SLOTS, 512], F32))
        ps_p = ctx.enter_context(nc.psum_tensor("ps_p", [P, 3, 512], F32))
        ps_n = ps_p
        G_FEAT, G_BIAS, G_OUT = (slice(k * WINDOW, (k + 1) * WINDOW) for k in range(3))

        s_rowsrc = sem("s_rowsrc")
        s_code_steps = sem("s_code_steps")
        s_code = sem("s_code")
        s_code_out = sem("s_code_out")
        s_codes = [sem(f"s_codes{j}") for j in range(SLOTS)]
        s_split = sem("s_split")
        s_hot = sem("s_hot")
        s_pick = sem("s_pick")
        s_masked = sem("s_masked")
        s_picked = sem("s_picked")
        s_weights = sem("s_weights")
        s_x = sem("s_x")
        s_dst = sem("s_dst")
        s_const = sem("s_const")
        s_iota = sem("s_iota")
        s_ln = sem("s_ln")
        s_ln_std = sem("s_ln_std")
        s_prep = sem("s_prep")
        s_ends_t = sem("s_ends_t")
        s_ends_b = sem("s_ends_b")
        s_bases = sem("s_bases")
        s_table = sem("s_table")
        s_rows = sem("s_rows")
        s_turn = sem("s_turn")
        s_turned = sem("s_turned")
        s_src = [sem(f"s_src{j}") for j in range(SLOTS)]
        s_attr = [sem(f"s_attr{j}") for j in range(SLOTS)]
        s_gath = [sem(f"s_gath{j}") for j in range(SLOTS)]
        s_form = sem("s_form")
        s_g = sem("s_g")
        s_gcopy = sem("s_gcopy")
        s_agg = sem("s_agg")
        s_add = sem("s_add")
        s_bn = sem("s_bn")
        s_bn_std = sem("s_bn_std")
        s_bn_done = sem("s_bn_done")
        s_relu = sem("s_relu")
        s_out = sem("s_out")
        s_fin = sem("s_fin")
        w_src, w_attr, w_gath, w_rows = sem("w_src"), sem("w_attr"), sem("w_gath"), sem("w_rows")
        w_go_sp, w_form, w_g, w_copy, w_agg = (sem("w_go_sp"), sem("w_form"), sem("w_g"),
                                                sem("w_copy"), sem("w_agg"))
        w_go_pool, w_iota, w_prod, w_add = sem("w_go_pool"), sem("w_iota"), sem("w_prod"), sem("w_add")
        s_start = sem("s_start")
        s_whole = sem("s_whole")

        rows_of = lambda t: t.rearrange("(p j) d -> p j d", j=COLS)
        by_col = nodes[:, 0:N].rearrange("q (p j) -> q j p", j=COLS)
        by_row = nodes[:, 0:N].rearrange("q (p j) -> q p j", j=COLS)

        TURNS_IN = COLS // PER_T
        TURNS_OUT = COLS // PER_R

        def turns_before(layer):
            return TURNS_IN + layer * (NBLOCKS + TURNS_OUT)

        def further_windows(eng, engine_type, body):
            n = nc.values_load(further_i[0:1, 0:1], engines=(engine_type,), min_val=0,
                               max_val=FURTHER,
                               skip_runtime_bounds_check_because="a sum of FURTHER zeros or ones")
            with eng.If(n > 0):
                with eng.Fori(0, n) as w:
                    body.window(w)
                    with eng.Fori(0, CHUNKS) as c:
                        body.chunk(w, c)
            with eng.Else():
                eng.nop()

        class Body:
            def __init__(self, window, chunk):
                self.window, self.chunk = window, chunk

        def taken(eng, s, n):
            eng.wait_ge(s, n)
            eng.sem_clear(s)

        def ends_bank(m, k):
            n = m * SLOTS + k
            return ps_g[:, n // 2, n % 2 * P:(n % 2 + 1) * P]

        def unit_bank(u):
            same = [k for k in range(UNITS) if k % 3 == u % 3]
            n = same.index(u)
            return u % 3, (u - same[n - 1] if n else u - same[-1] + UNITS)

        def rounds(eng, step, drain=()):
            for j in range(SLOTS):
                step(0, j, True, False)
            with eng.Fori(1, ROUNDS - 1) as r:
                for j in range(SLOTS):
                    step(r, j, False, False)
            for j in range(SLOTS):
                step(ROUNDS - 1, j, False, True)

        def ahead(r, j, last, n):
            if j + n < SLOTS:
                return r, j + n
            return None if last else (r + 1, j + n - SLOTS)

        block = ctx.enter_context(nc.Block())

        @block.sync
        def _(sp):
            sp.dma_start(x_rows[:], rows_of(x)).then_inc(s_x, 16)
            for j in range(SLOTS):
                sp.dma_start(src_s[j][:], src[j]).then_inc(s_src[j], 16)
                sp.dma_start(attr_s[j][:], edge_attr[j].rearrange("p (t f) -> p t f", t=TILES)) \
                  .then_inc(s_attr[j], 16)
            sp.dma_start(dst_i[:], dst).then_inc(s_dst, 16)
            for tile, view in (
                (w_feat[:], edge_w.rearrange("l f (i o) -> (f i) l o", o=D)),
                (w_bias[:], edge_b.rearrange("l (i o) -> i l o", o=D)),
                (w_root[:], root_w.rearrange("l i o -> i l o")),
                (b_root[:], root_bt), (gamma[:], gamma_t), (beta[:], beta_t),
                (w_pred[:], pred_w), (b_pred[:], pred_b.to_broadcast([ROWS, D])),
            ):
                sp.dma_start(tile, view).then_inc(s_weights, 16)

            sp.dma_start(src_i[:], src_rows.rearrange("(b c) e -> b c e", c=CROWS)).then_inc(s_rowsrc, 16)
            sp.dma_start(cols_i[:], src_cols).then_inc(s_rowsrc, 16)

            def load_codes(c, j):
                n = PICKS[j] * P
                if n:
                    sp.dma_start(code_s[j][:, 0:PICKS[j], :].rearrange("b k e -> b (k e)"),
                                 code_table[c, 0:n].to_broadcast([ROWS, n])).then_inc(s_codes[j], 16)

            for layer in range(LAYERS):
                done = layer * CHUNKS
                sp.wait_ge(s_rows, layer + 1 if layer == 0 else 1 + layer * TURNS_OUT)
                sp.dma_start(rows_of(h_table), h_rows[:]).then_inc(s_table, 16)
                if layer == 0:
                    sp.wait_ge(s_code, 1)
                    sp.dma_start(code_table.rearrange("(b c) e -> b c e", c=CROWS), code[:]).then_inc(s_code_out, 16)
                    sp.wait_ge(s_code_out, 16)
                for j in range(SLOTS):
                    load_codes(slice(j, j + 1), j)

                def refill(c, j):
                    sp.wait_ge(s_g, c - SLOTS + 1 + done)
                    sp.dma_start(src_s[j][:], src[bass.ds(c, 1)].rearrange("a p t -> (a p) t")) \
                      .then_inc(s_src[j], 16)
                    load_codes(bass.ds(c, 1), j)
                    sp.dma_start(attr_s[j][:], edge_attr[bass.ds(c, 1)].rearrange("a p (t f) -> (a p) t f", t=TILES)) \
                      .then_inc(s_attr[j], 16)

                with sp.Fori(1, ROUNDS) as r:
                    for j in range(SLOTS):
                        refill(r * SLOTS + j, j)

                def window(w):
                    pass

                def chunk(w, c):
                    taken(sp, w_go_sp, 1)
                    sp.dma_start(src_s[0][:], src[bass.ds(c, 1)].rearrange("a p t -> (a p) t")).then_inc(w_src, 16)
                    sp.dma_start(attr_s[0][:], edge_attr[bass.ds(c, 1)].rearrange("a p (t f) -> (a p) t f", t=TILES)).then_inc(w_attr, 16)

                sp.wait_ge(s_bases, 1)
                sp.wait_ge(s_form, (done + CHUNKS) * 2)
                further_windows(sp, mybir.EngineType.SP, Body(window, chunk))
                if layer < LAYERS - 1:
                    sp.wait_ge(s_whole, layer + 1)
                    for j in range(SLOTS):
                        sp.dma_start(src_s[j][:], src[j]).then_inc(s_src[j], 16)
                        sp.dma_start(attr_s[j][:], edge_attr[j].rearrange("p (t f) -> p t f", t=TILES)) \
                          .then_inc(s_attr[j], 16)

            sp.wait_ge(s_fin, 2 * TURNS_OUT)
            sp.dma_start(rows_of(out), h_rows[:]).then_inc(s_out, 16)
            sp.wait_ge(s_out, 16)

        @block.gpsimd
        def _(pool):
            pool.memset(ident[:], 0.0).then_inc(s_const, 1)
            pool.memset(ones[:], 1.0).then_inc(s_const, 1)
            pool.iota(iota_i[:], pattern=[[1, WIDE]], base=0, channel_multiplier=0).then_inc(s_const, 1)
            pool.iota(rowpart_i[:], pattern=[[1, PARTS]], base=0, channel_multiplier=PARTS).then_inc(s_const, 1)
            pool.wait_ge(s_const, 4)
            pool.affine_select(out=ident[:], in_=ident[:], compare_op=ALU.not_equal, fill=1.0,
                               base=0, pattern=[[-1, P]], channel_multiplier=1).then_inc(s_const, 1)

            def gather(j, signal, first_tile):
                for t in range(first_tile, TILES):
                    pool.indirect_dma_start(
                        out=h_src[j][:, t, :], out_offset=None, in_=h_table,
                        in_offset=bass.IndirectOffsetOnAxis(ap=src_s[j][:, t:t + 1], axis=0)
                    ).then_inc(signal, 16)

            for layer in range(LAYERS):
                done = layer * CHUNKS
                pool.wait_ge(s_table, 16 * (layer + 1))

                def step(r, j, first):
                    c = r * SLOTS + j
                    pool.wait_ge(s_src[j], (r + 1 + layer * ROUNDS) * 16)
                    pool.sem_inc(s_start, 1)
                    gather(j, s_gath[j], PICKS[j])

                for j in range(SLOTS):
                    step(0, j, True)
                with pool.Fori(1, ROUNDS) as r:
                    for j in range(SLOTS):
                        step(r, j, False)

                def chunk(w, c):
                    taken(pool, w_go_pool, 1)
                    taken(pool, w_src, 16)
                    gather(0, w_gath, 0)
                    pool.wait_ge(w_gath, 16 * TILES)
                    pool.dma_reset(range(w_gath.num, w_gath.num + 1))
                    pool.sem_clear(w_gath)
                    pool.sem_inc(w_rows, 1)

                pool.wait_ge(s_bases, 1)
                pool.wait_ge(s_g, done + CHUNKS)
                further_windows(pool, mybir.EngineType.Pool, Body(lambda w: None, chunk))

        @block.tensor
        def _(pe):
            mm = nc.tensor.matmul
            pe.wait_ge(s_const, 5)
            pe.wait_ge(s_rows, 1)
            for k in range(TURNS_IN):
                if k >= 2:
                    pe.wait_ge(s_turned, k - 1)
                for q in range(PER_T):
                    last = nc.tensor.transpose(ps_n[0:D, k % 2, q * ROWS:(q + 1) * ROWS],
                                               h_rows[:, k * PER_T + q, :], ident[0:ROWS, 0:ROWS])
                last.then_inc(s_turn, 1)
            pe.wait_ge(s_prep, 3)
            for k in range(SLOTS):
                for m in range(2):
                    last = nc.tensor.transpose(ends_bank(m, k)[0:BLOCK, :],
                                               chunk_ends[:, m, k * BLOCK:(k + 1) * BLOCK], ident[:])
            last.then_inc(s_ends_t, 1)
            pe.wait_ge(s_prep, 6)
            for k in range(SLOTS):
                for m in range(2):
                    last = mm(ends_bank(m, k)[:, 0:BLOCK], ones[0:BLOCK, :],
                              ends_diag[:, m, k, :], start=True, stop=True)
            last.then_inc(s_ends_b, 1)
            pe.wait_ge(s_weights, 8 * 16)

            def reduce_chunk(feat, bias, h, z, hot):
                for t in range(TILES):
                    mm(feat, z[:, t, :, :].rearrange("p f i -> p (f i)"), hot[:, t, :],
                       start=(t == 0), stop=(t == TILES - 1))
                for t in range(TILES):
                    last = mm(bias, h[:, t, :], hot[:, t, :], start=(t == 0), stop=(t == TILES - 1))
                return last

            def apply_w(layer, to, feat, bias):
                mm(to, w_feat[:, layer, :], feat, start=True, stop=False)
                return mm(to, w_bias[:, layer, :], bias, start=False, stop=True)

            for layer in range(LAYERS):
                done = layer * CHUNKS
                before = turns_before(layer)
                for b in range(NBLOCKS):
                    n = before + b
                    pe.wait_ge(s_turned, n if layer == 0 and b == 0 else n - 1)
                    mm(ps_n[0:D, n % 2, 0:NB], w_root[:, layer, :], nodes[:, b * NB:(b + 1) * NB],
                       start=True, stop=True).then_inc(s_turn, 1)
                if layer == 0:
                    pe.wait_ge(s_bases, 1)

                def pick_step(r, j, first):
                    c = r * SLOTS + j
                    if not PICKS[j]:
                        return
                    pe.wait_ge(s_hot, c + 1 + done)
                    for k in range(PICKS[j]):
                        u = FIRST_UNIT[j] + k
                        bank, before_it = unit_bank(u)
                        if not (first and u < before_it):
                            pe.wait_ge(s_masked, r * UNITS + u + 1 - before_it + layer * ROUNDS * UNITS)
                        for m in range(PARTS):
                            for h in range(SPLITS):
                                last = mm(ps_p[:, bank, 0:PART * D], pick_hot[j][:, k, m, :], h_split[:, h, m, :],
                                          start=(m == 0 and h == 0), stop=(m == PARTS - 1 and h == SPLITS - 1))
                        last.then_inc(s_pick, 1)

                def reduce_step(r, j, first):
                    c = r * SLOTS + j
                    pe.wait_ge(s_form, (c + 1 + done) * 2)
                    if not (first and layer == 0):
                        pe.wait_ge(s_add, c - SLOTS + 1 + done)
                    reduce_chunk(ps_g[:, j, G_FEAT], ps_g[0:D, j, G_BIAS],
                                 h_src[j], prod[j], onehot[j]).then_inc(s_g, 1)

                def apply_step(r, j, first):
                    c = r * SLOTS + j
                    pe.wait_ge(s_gcopy, (c + 1 + done) * 2)
                    apply_w(layer, ps_g[0:D, j, G_OUT], g_feat[j][:],
                            g_bias[j][:]).then_inc(s_agg, 1)

                def step(r, j, first, last):
                    if then := ahead(r, j, last, 2):
                        pick_step(*then, first and j + 2 < SLOTS)
                    reduce_step(r, j, first)
                    if j:
                        apply_step(r, j - 1, first)
                    elif not first:
                        apply_step(r - 1, SLOTS - 1, False)

                pe.wait_ge(s_split, 5 * (layer + 1))
                pe.wait_ge(s_turned, before + NBLOCKS)
                pick_step(0, 0, True)
                pick_step(0, 1, True)
                rounds(pe, step)
                apply_step(ROUNDS - 1, SLOTS - 1, False)

                def chunk(w, c):
                    taken(pe, w_form, 2)
                    reduce_chunk(ps_g[:, 0, :], ps_g[0:D, 1, :], h_src[0], prod[0], wide_hot).then_inc(w_g, 1)
                    taken(pe, w_copy, 2)
                    apply_w(layer, ps_g[0:D, 2, :], wide_feat[:], wide_bias[:]).then_inc(w_agg, 1)

                pe.wait_ge(s_gcopy, 2 * (done + CHUNKS))
                pe.wait_ge(s_add, done + CHUNKS)
                further_windows(pe, mybir.EngineType.PE, Body(lambda w: None, chunk))

                if layer < LAYERS - 1:
                    for k in range(TURNS_OUT):
                        n = before + NBLOCKS + k
                        pe.wait_ge(s_relu, layer * TURNS_OUT + k + 1)
                        pe.wait_ge(s_turned, n - 1)
                        for q in range(PER_R):
                            last = nc.tensor.transpose(ps_n[0:ROWS, n % 2, q * D:(q + 1) * D],
                                                       by_col[:, k * PER_R + q, :], ident[0:D, 0:D])
                        last.then_inc(s_turn, 1)
                else:
                    for k in range(TURNS_OUT):
                        n = before + NBLOCKS + k
                        pe.wait_ge(s_relu, layer * TURNS_OUT + k + 1)
                        if k >= 2:
                            pe.wait_ge(s_fin, 2 * (k - 1))
                        else:
                            pe.wait_ge(s_turned, n - k)
                        for q in range(PER_R):
                            last = mm(ps_n[0:ROWS, n % 2, q * D:(q + 1) * D],
                                      by_col[:, k * PER_R + q, :], w_pred[:], start=True, stop=True)
                        last.then_inc(s_turn, 1)

        @block.scalar
        def _(act):
            copy = lambda o, i: nc.scalar.activation(o, i, ACT.Copy)
            act.wait_ge(s_ln, 6)
            nc.scalar.activation(ln_b[:], ln_a[:], ACT.Sqrt).then_inc(s_ln_std, 1)
            for k in range(TURNS_IN):
                act.wait_ge(s_turn, k + 1)
                copy(by_col[:, k * PER_T:(k + 1) * PER_T, :],
                     ps_n[0:D, k % 2, 0:NB].rearrange("q (j p) -> q j p", p=ROWS)).then_inc(s_turned, 1)
            act.wait_ge(s_weights, 8 * 16)

            for layer in range(LAYERS):
                done = layer * CHUNKS
                before = turns_before(layer)
                for b in range(NBLOCKS):
                    n = before + b
                    act.wait_ge(s_turn, n + 1)
                    nc.scalar.activation(nodes[:, b * NB:(b + 1) * NB], ps_n[0:D, n % 2, 0:NB],
                                         ACT.Identity, bias=b_root[:, layer:layer + 1]).then_inc(s_turned, 1)

                def step(r, j, first):
                    c = r * SLOTS + j
                    act.wait_ge(s_g, c + 1 + done)
                    if not (first and layer == 0):
                        act.wait_ge(s_agg, c - SLOTS + 1 + done)
                    copy(g_feat[j][:], ps_g[:, j, G_FEAT]).then_inc(s_gcopy, 1)
                    copy(g_bias[j][:], ps_g[0:D, j, G_BIAS]).then_inc(s_gcopy, 1)

                for j in range(SLOTS):
                    step(0, j, True)
                with act.Fori(1, ROUNDS) as r:
                    for j in range(SLOTS):
                        step(r, j, False)

                def chunk(w, c):
                    taken(act, w_g, 1)
                    copy(wide_feat[:], ps_g[:, 0, :]).then_inc(w_copy, 1)
                    copy(wide_bias[:], ps_g[0:D, 1, :]).then_inc(w_copy, 1)

                act.wait_ge(s_bases, 1)
                further_windows(act, mybir.EngineType.Activation, Body(lambda w: None, chunk))

                if layer < LAYERS - 1:
                    act.wait_ge(s_bn, (layer + 1) * (NBLOCKS + 2))
                    nc.scalar.activation(bn_s[:, 1:2], bn_s[:, 0:1], ACT.Sqrt).then_inc(s_bn_std, 1)
                    act.wait_ge(s_bn_done, 4 * (layer + 1))
                else:
                    act.wait_ge(s_whole, LAYERS)
                scale = bn_s[:, 2:3] if layer < LAYERS - 1 else 1.0
                shift = bn_s[:, 3:4] if layer < LAYERS - 1 else 0.0

                def relu(k):
                    part = by_row[:, :, k * PER_R:(k + 1) * PER_R]
                    nc.scalar.activation(part, part, ACT.Relu, bias=shift, scale=scale).then_inc(s_relu, 1)

                relu(0)
                for k in range(TURNS_OUT):
                    if k + 1 < TURNS_OUT:
                        relu(k + 1)
                    if layer < LAYERS - 1:
                        n = before + NBLOCKS + k
                        act.wait_ge(s_turn, n + 1)
                        if k == 0:
                            act.wait_ge(s_table, 16 * (layer + 1))
                        copy(h_rows[:, k * PER_R:(k + 1) * PER_R, :].rearrange("p j d -> p (j d)"),
                             ps_n[0:ROWS, n % 2, 0:PER_R * D]).then_inc(s_turned, 1)
                        act.wait_ge(s_turned, n + 1)
                        act.sem_inc(s_rows, 1)

        @block.vector
        def _(dve):
            v = nc.vector
            dve.wait_ge(s_x, 16)
            wide = lambda t: t[:].unsqueeze(2).to_broadcast([ROWS, COLS, D])
            v.tensor_reduce(ln_a[:], x_rows[:], AX.X, ALU.add).then_inc(s_ln, 1)
            dve.wait_ge(s_ln, 1)
            v.tensor_scalar(ln_b[:], ln_a[:], 1.0 / D, None, ALU.mult).then_inc(s_ln, 1)
            dve.wait_ge(s_ln, 2)
            v.tensor_tensor(h_rows[:], x_rows[:], wide(ln_b), ALU.subtract).then_inc(s_ln, 1)
            dve.wait_ge(s_ln, 3)
            squares = ln_sq[:]
            v.tensor_tensor(squares, h_rows[:], h_rows[:], ALU.mult).then_inc(s_ln, 1)
            dve.wait_ge(s_ln, 4)
            v.tensor_reduce(ln_b[:], squares, AX.X, ALU.add).then_inc(s_ln, 1)
            dve.wait_ge(s_ln, 5)
            v.tensor_scalar(ln_a[:], ln_b[:], 1.0 / D, LN_EPS, ALU.mult, ALU.add).then_inc(s_ln, 1)
            dve.wait_ge(s_ln_std, 1)
            v.reciprocal(ln_a[:], ln_b[:]).then_inc(s_ln, 1)
            dve.wait_ge(s_ln, 7)
            v.tensor_tensor(h_rows[:], h_rows[:], wide(ln_a), ALU.mult).then_inc(s_ln, 1)
            dve.wait_ge(s_ln, 8)
            v.tensor_scalar(h_rows[:], h_rows[:], 0.0, None, ALU.max).then_inc(s_rows, 1)

            by_part = (1.0 / PART, -(PART - 1) / (2.0 * PART), ALU.mult, ALU.add)
            code_f = ln_sq[0:BLOCK].rearrange("b j d -> b (j d)")[:, 0:CROWS * PICKED * P]
            flat = lambda t: t[:].rearrange("b c e -> b (c e)")
            dve.wait_ge(s_rowsrc, 32)
            v.tensor_scalar(code_f, flat(src_i), *by_part).then_inc(s_code_steps, 1)
            dve.wait_ge(s_code_steps, 1)
            v.tensor_scalar(flat(code), code_f, ROUND, -ROUND, ALU.add, ALU.add).then_inc(s_code, 1)
            v.tensor_scalar(cols_q[:], cols_i[:], *by_part).then_inc(s_code_steps, 1)
            dve.wait_ge(s_code_steps, 2)
            v.tensor_scalar(cols_q[:], cols_q[:], ROUND, -ROUND, ALU.add, ALU.add).then_inc(s_code_steps, 1)
            dve.wait_ge(s_code_steps, 3)
            v.scalar_tensor_tensor(rest[:], cols_q[:], -float(PART), cols_i[:], ALU.mult, ALU.add).then_inc(s_code_steps, 1)

            dve.wait_ge(s_const, 5)
            v.tensor_copy(iota[:], iota_i[:]).then_inc(s_iota, 1)
            v.tensor_copy(rowpart[:], rowpart_i[:]).then_inc(s_code_steps, 1)
            v.memset(nodes[:, N:N + WIDE], 0.0)
            dve.wait_ge(s_dst, 16)
            v.tensor_copy(dst_rel[:], dst_i[:]).then_inc(s_prep, 1)
            dve.wait_ge(s_prep, 1)
            v.tensor_reduce(chunk_ends[:, 0, :], dst_rel[:], AX.X, ALU.min).then_inc(s_prep, 1)
            v.tensor_reduce(chunk_ends[:, 1, :], dst_rel[:], AX.X, ALU.max).then_inc(s_prep, 1)
            dve.wait_ge(s_ends_t, 1)
            for m, op in enumerate((ALU.min, ALU.max)):
                for k in range(SLOTS):
                    last = v.tensor_reduce(ends_col[:, m, k:k + 1], ends_bank(m, k)[0:BLOCK, :], AX.X, op)
                last.then_inc(s_prep, 1)
            dve.wait_ge(s_prep, 5)
            v.tensor_tensor(
                ends_diag[:].rearrange("p m k c -> p (m k) c"),
                ends_col[:].rearrange("p m k -> p (m k)").unsqueeze(2).to_broadcast([BLOCK, 2 * SLOTS, BLOCK]),
                ident[0:BLOCK, 0:BLOCK].unsqueeze(1).to_broadcast([BLOCK, 2 * SLOTS, BLOCK]),
                ALU.mult).then_inc(s_prep, 1)
            dve.wait_ge(s_ends_b, 1)
            for m in range(2):
                for k in range(SLOTS):
                    last = v.tensor_copy(ends_row[:, m, k * BLOCK:(k + 1) * BLOCK], ends_bank(m, k)[:, 0:BLOCK])
                last.then_inc(s_prep, 1)
            dve.wait_ge(s_prep, 8)
            v.tensor_tensor(dst_rel[:], dst_rel[:], ends_row[:, 0, :].unsqueeze(2).to_broadcast([P, CHUNKS, TILES]),
                            ALU.subtract).then_inc(s_prep, 1)
            v.tensor_copy(base_i[:], ends_row[0:1, 0, :]).then_inc(s_prep, 1)
            v.tensor_tensor(span[:], ends_row[0:1, 1, :], ends_row[0:1, 0, :], ALU.subtract).then_inc(s_prep, 1)
            dve.wait_ge(s_prep, 11)
            dve.wait_ge(s_iota, 1)
            v.tensor_reduce(span_max[:], span[:], AX.X, ALU.max).then_inc(s_prep, 1)
            v.tensor_scalar(further[:], iota[0:1, 0:FURTHER], float(WIDE), float(WINDOW), ALU.mult, ALU.add) \
                .then_inc(s_prep, 1)
            dve.wait_ge(s_prep, 13)
            v.tensor_scalar(further[:], further[:], span_max[:], None, ALU.is_le).then_inc(s_prep, 1)
            dve.wait_ge(s_prep, 14)
            v.tensor_reduce(further_n[:], further[:], AX.X, ALU.add).then_inc(s_prep, 1)
            dve.wait_ge(s_prep, 15)
            v.tensor_copy(further_i[:], further_n[:]).then_inc(s_bases, 1)
            dve.wait_ge(s_bases, 1)

            def products(j):
                return v.tensor_tensor(
                    prod[j][:],
                    attr_s[j][:].unsqueeze(3).to_broadcast([P, TILES, FEAT, D]),
                    h_src[j][:].unsqueeze(2).to_broadcast([P, TILES, FEAT, D]), ALU.mult)

            def one_hots(hot, c, row, width):
                return v.tensor_tensor(
                    hot[:], dst_rel[:, bass.ds(c, 1), :].rearrange("p a t -> p (a t)").unsqueeze(2).to_broadcast([P, TILES, width]),
                    row.unsqueeze(1).to_broadcast([P, TILES, width]), ALU.is_equal)

            for layer in range(LAYERS):
                done = layer * CHUNKS

                dve.wait_ge(s_rows, 1 + layer * TURNS_OUT)
                left, n_split = h_rows, 5 * layer
                for h in range(SPLITS):
                    part = h_split[:, h, :, :].rearrange("b m c -> b (m c)")
                    whole = left[:].rearrange("b j d -> b (j d)")
                    v.tensor_copy(part, whole).then_inc(s_split, 1)
                    n_split += 1
                    dve.wait_ge(s_split, n_split)
                    if h < SPLITS - 1:
                        v.tensor_tensor(h_left[:].rearrange("b j d -> b (j d)"), whole, part, ALU.subtract) \
                            .then_inc(s_split, 1)
                        n_split += 1
                        dve.wait_ge(s_split, n_split)
                    left = h_left

                def hot_step(r, j, first):
                    c = r * SLOTS + j
                    n = PICKS[j]
                    if not n:
                        return
                    dve.wait_ge(s_codes[j], (r + 1 + layer * ROUNDS) * 16)
                    if not (first and layer == 0):
                        dve.wait_ge(s_g, c - SLOTS + 1 + done)
                    v.tensor_tensor(
                        pick_hot[j][:, 0:n].rearrange("b k m e -> b k m e"),
                        code_s[j][:, 0:n, :].unsqueeze(2).to_broadcast([ROWS, n, PARTS, P]),
                        rowpart[0:ROWS, :].unsqueeze(1).unsqueeze(3).to_broadcast([ROWS, n, PARTS, P]),
                        ALU.is_equal).then_inc(s_hot, 1)

                def pick_step(r, j, first):
                    c = r * SLOTS + j
                    for k in range(PICKS[j]):
                        u = FIRST_UNIT[j] + k
                        n = r * UNITS + u + layer * ROUNDS * UNITS
                        bank, before_it = unit_bank(u)
                        dve.wait_ge(s_pick, n + 1)
                        if not (first and u < before_it):
                            dve.wait_ge(s_picked, n + 1 - before_it)
                        to = picked[bank]
                        v.scalar_tensor_tensor(
                            to[:], iota[:, 0:PART].unsqueeze(1).to_broadcast([P, D, PART]),
                            rest[:, bass.ds(c, 1), k],
                            ps_p[:, bank, 0:PART * D].rearrange("p (s d) -> p d s", d=D),
                            ALU.is_equal, ALU.mult).then_inc(s_masked, 1)
                        dve.wait_ge(s_masked, n + 1)
                        v.tensor_reduce(h_src[j][:, k, :], to[:], AX.X, ALU.add).then_inc(s_picked, 1)

                def form_step(r, j, first):
                    c = r * SLOTS + j
                    if not (first and layer == 0):
                        dve.wait_ge(s_g, c - SLOTS + 1 + done)
                    one_hots(onehot[j], c, iota[:, 0:WINDOW], WINDOW).then_inc(s_form, 1)
                    dve.wait_ge(s_attr[j], (r + 1 + layer * ROUNDS) * 16)
                    dve.wait_ge(s_gath[j], (r + 1 + layer * ROUNDS) * 16 * (TILES - PICKS[j]))
                    if PICKS[j]:
                        dve.wait_ge(s_picked, r * UNITS + FIRST_UNIT[j] + PICKS[j] + layer * ROUNDS * UNITS)
                    products(j).then_inc(s_form, 1)

                def add_step(r, j, first, base):
                    c = r * SLOTS + j
                    dve.wait_ge(s_agg, c + 1 + done)
                    if not (first and layer == 0 and j == 0):
                        dve.wait_ge(s_add, c + done)
                    at = nodes[:, bass.ds(base, WINDOW)]
                    v.tensor_tensor(at, at, ps_g[0:D, j, G_OUT], ALU.add).then_inc(s_add, 1)

                def base_of(c):
                    return nc.values_load(base_i[0:1, bass.ds(c, 1)], engines=(DVE,), min_val=0,
                                          max_val=N, skip_runtime_bounds_check_because="a node's number")

                def step(r, j, first, last):
                    if then := ahead(r, j, last, 2):
                        hot_step(*then, first and j + 2 < SLOTS)
                    if then := ahead(r, j, last, 1):
                        pick_step(*then, first and j + 1 < SLOTS)
                    form_step(r, j, first)
                    if first and j == 0:
                        dve.wait_ge(s_turned, turns_before(layer) + NBLOCKS)
                    if j >= 2:
                        add_step(r, j - 2, first, base_of(r * SLOTS + j - 2))
                    elif not first:
                        add_step(r - 1, j - 2 + SLOTS, False, base_of(r * SLOTS + j - 2))

                dve.wait_ge(s_code_steps, 5)
                hot_step(0, 0, True)
                hot_step(0, 1, True)
                pick_step(0, 0, True)
                rounds(dve, step)
                for j in (SLOTS - 2, SLOTS - 1):
                    add_step(ROUNDS - 1, j, False, base_of((ROUNDS - 1) * SLOTS + j))
                dve.wait_ge(s_add, done + CHUNKS)

                v.tensor_scalar(iota_w[:], iota[:], float(WINDOW - WIDE), None, ALU.add).then_inc(w_iota, 1)
                dve.sem_inc(w_add, 1)

                def window(w):
                    taken(dve, w_iota, 1)
                    v.tensor_scalar(iota_w[:], iota_w[:], float(WIDE), None, ALU.add).then_inc(w_iota, 1)

                def chunk(w, c):
                    dve.sem_inc(w_go_sp, 1)
                    dve.sem_inc(w_go_pool, 1)
                    dve.wait_ge(w_iota, 1)
                    one_hots(wide_hot, c, iota_w[:], WIDE).then_inc(w_form, 1)
                    taken(dve, w_attr, 16)
                    taken(dve, w_rows, 1)
                    products(0).then_inc(w_form, 1)
                    base = nc.values_load(base_i[0:1, bass.ds(c, 1)], engines=(DVE,), min_val=0,
                                          max_val=N - 1, skip_runtime_bounds_check_because="a node's number")
                    start = dve.snap(base + w * WIDE + WINDOW)
                    clamped = nc.s_assert_within(start - (start - N) * (start > N), 0, N,
                                                 skip_runtime_bounds_check_because="cut off at N")
                    taken(dve, w_agg, 1)
                    at = nodes[:, bass.ds(clamped, WIDE)]
                    taken(dve, w_add, 1)
                    v.tensor_tensor(at, at, ps_g[0:D, 2, :], ALU.add).then_inc(w_add, 1)
                    dve.wait_ge(w_add, 1)

                further_windows(dve, DVE, Body(window, chunk))
                taken(dve, w_iota, 1)
                taken(dve, w_add, 1)
                dve.sem_inc(s_whole, 1)

                if layer < LAYERS - 1:
                    for b in range(NBLOCKS):
                        v.bn_stats(bn_parts[:, b, :], nodes[:, b * NB:(b + 1) * NB]).then_inc(s_bn, 1)
                    before = layer * (NBLOCKS + 2)
                    dve.wait_ge(s_bn, before + NBLOCKS)
                    v.bn_aggr(bn_mv[:], bn_parts[:].rearrange("q b s -> q (b s)")).then_inc(s_bn, 1)
                    dve.wait_ge(s_bn, before + NBLOCKS + 1)
                    v.tensor_scalar(bn_s[:, 0:1], bn_mv[:, 1:2], BN_EPS, None, ALU.add).then_inc(s_bn, 1)
                    dve.wait_ge(s_bn_std, layer + 1)
                    v.reciprocal(bn_s[:, 2:3], bn_s[:, 1:2]).then_inc(s_bn_done, 1)
                    dve.wait_ge(s_bn_done, 4 * layer + 1)
                    v.tensor_tensor(bn_s[:, 2:3], bn_s[:, 2:3], gamma[:, layer:layer + 1], ALU.mult).then_inc(s_bn_done, 1)
                    dve.wait_ge(s_bn_done, 4 * layer + 2)
                    v.tensor_tensor(bn_s[:, 3:4], bn_mv[:, 0:1], bn_s[:, 2:3], ALU.mult).then_inc(s_bn_done, 1)
                    dve.wait_ge(s_bn_done, 4 * layer + 3)
                    v.tensor_tensor(bn_s[:, 3:4], beta[:, layer:layer + 1], bn_s[:, 3:4], ALU.subtract).then_inc(s_bn_done, 1)

            dve.wait_ge(s_table, 16 * LAYERS)
            for k in range(TURNS_OUT):
                n = turns_before(LAYERS - 1) + NBLOCKS + k
                dve.wait_ge(s_turn, n + 1)
                rows = h_rows[:, k * PER_R:(k + 1) * PER_R, :]
                v.tensor_tensor(rows, ps_n[0:ROWS, n % 2, 0:PER_R * D].rearrange("p (j d) -> p j d", d=D),
                                b_pred[:].unsqueeze(1).to_broadcast([ROWS, PER_R, D]), ALU.add).then_inc(s_fin, 1)
                dve.wait_ge(s_fin, 2 * k + 1)
                v.tensor_tensor(rows, rows, x_rows[:, k * PER_R:(k + 1) * PER_R, :], ALU.add).then_inc(s_fin, 1)


def kernel(**inputs):
    import numpy as np
    import concourse.bacc as bacc
    from concourse.bass_utils import run_bass_kernel_spmd

    def edges_by_chunk(a):
        return np.ascontiguousarray(np.asarray(a).reshape(-1, P, TILES * (a.shape[1] if a.ndim > 1 else 1)))

    arrays = {
        "x": inputs["x"],
        "src": edges_by_chunk(inputs["src"]),
        "src_rows": np.asarray(inputs["src"]).reshape(-1, P, TILES)[:, :, :PICKED].transpose(0, 2, 1)
                      .reshape(-1, PICKED * P),
        "src_cols": np.asarray(inputs["src"]).reshape(-1, P, TILES)[:, :, :PICKED].transpose(1, 0, 2),
        "dst": np.asarray(inputs["dst"]).reshape(-1, P, TILES).transpose(1, 0, 2),
        "edge_attr": edges_by_chunk(inputs["edge_attr_8"]),
        "edge_w": inputs["L0_gnn_edge_w"],
        "edge_b": inputs["L0_gnn_edge_b"],
        "root_w": inputs["L0_gnn_root_w"],
        "root_bt": np.asarray(inputs["L0_gnn_root_b"]).T,
        "gamma_t": np.asarray(inputs["L0_gnn_bn_gamma"]).T,
        "beta_t": np.asarray(inputs["L0_gnn_bn_beta"]).T,
        "pred_w": inputs["L0_gnn_pred_w"],
        "pred_b": np.asarray(inputs["L0_gnn_pred_b"]).reshape(1, -1),
    }
    arrays = {f"in_{k}": np.ascontiguousarray(a) for k, a in arrays.items()}
    nc = bacc.Bacc("TRN2", target_bir_lowering=False, num_devices=1)
    args = [nc.dram_tensor(k, a.shape, mybir.dt.from_np(a.dtype), kind="ExternalInput").ap()
            for k, a in arrays.items()]
    out = nc.dram_tensor("out", inputs["x"].shape, F32, kind="ExternalOutput").ap()
    gnn(nc, *args, out)
    r = run_bass_kernel_spmd(nc, [arrays], core_ids=[0])
    return r.results[0]["out"]
```

```python
import concourse.bass as bass
from concourse import mybir

F32 = mybir.dt.float32
I32 = mybir.dt.int32
F16 = mybir.dt.float16
F32R = mybir.dt.float32r
ALU = mybir.AluOpType
ACT = mybir.ActivationFunctionType
AX = mybir.AxisListType
DVE = mybir.EngineType.DVE
ENGINES = (mybir.EngineType.Pool, mybir.EngineType.Activation, mybir.EngineType.PE,
           mybir.EngineType.DVE, mybir.EngineType.SP)

P = 128
TILES = 5
SLOTS = 5
WINDOW = 48
WIDE = 512
LN_EPS = 1e-5
BN_EPS = 1e-5


PICKS = [2, 1, 2, 1, 2]
PICKED = max(PICKS)
PARTS = 5
SPLITS = 2
ROUND = 1.5 * 2 ** 23


def gnn(nc, x, src, src_rows, src_cols, dst, edge_attr, edge_w, edge_b, root_w, root_bt, gamma_t, beta_t, pred_w,
        pred_b, out):
    N, D = x.shape
    CHUNKS = src.shape[0]
    FEAT = edge_attr.shape[2] // TILES
    FD = FEAT * D
    LAYERS = edge_w.shape[0]
    ROWS = 125
    COLS = N // ROWS
    BLOCK = CHUNKS // SLOTS
    ROUNDS = CHUNKS // SLOTS
    NB = 500
    NBLOCKS = N // NB
    PER_T = NB // ROWS
    PER_R = COLS // 4
    FURTHER = -(-(N - WINDOW) // WIDE)
    assert ROWS * COLS == N and NBLOCKS * NB == N and BLOCK <= P and CHUNKS % SLOTS == 0
    assert FD == P and src.shape[1:] == (P, TILES)

    PART = COLS // PARTS
    ROWN = ROWS * PARTS
    SPLIT_STEPS = 2 * SPLITS - 1
    UNITS = sum(PICKS)
    FIRST_UNIT = [sum(PICKS[:j]) for j in range(SLOTS)]
    MORE = [n - 1 for n in PICKS]
    FIRST_MORE = [sum(MORE[:j]) for j in range(SLOTS)]
    assert min(PICKS) > 0 and PICKED <= 2

    def more(r, j, layer):
        return (r + layer * ROUNDS) * sum(MORE) + FIRST_MORE[j] + MORE[j]
    CROWS = CHUNKS // BLOCK
    assert PARTS * PART == COLS and ROWN <= 2048 and PART * D <= 512

    code_table = nc.dram_tensor("code_table", (CHUNKS, PICKED * P), F16, kind="Internal").ap()
    h_table = nc.dram_tensor("h_table", (N, D), F32, kind="Internal").ap()

    from contextlib import ExitStack
    ctx = ExitStack()
    with ctx:
        def sb(name, shape, dt=F32):
            return ctx.enter_context(nc.sbuf_tensor(name, shape, dt))

        def sem(name):
            return ctx.enter_context(nc.semaphore(name))

        w_feat = sb("w_feat", [FD, LAYERS, D])
        w_bias = sb("w_bias", [2 * D, LAYERS, D])
        w_root = sb("w_root", [D, LAYERS, D])
        b_root = sb("b_root", [D, LAYERS])
        gamma = sb("gamma", [D, LAYERS - 1])
        beta = sb("beta", [D, LAYERS - 1])
        w_pred = sb("w_pred", [D, D])
        b_pred = sb("b_pred", [ROWS, D])
        ident = sb("ident", [P, P])
        ones = sb("ones", [P, P])
        iota_i = sb("iota_i", [P, WIDE], I32)
        iota = sb("iota", [P, WIDE])
        iota_w = sb("iota_w", [P, WIDE])
        x_rows = sb("x_rows", [ROWS, COLS, D])
        h_rows = sb("h_rows", [ROWS, COLS, D])
        nodes = sb("nodes", [D, N + WIDE])
        ln_a = sb("ln_a", [ROWS, COLS])
        ln_b = sb("ln_b", [ROWS, COLS])
        bn_parts = sb("bn_parts", [D, NBLOCKS, 6])
        bn_mv = sb("bn_mv", [D, 2])
        bn_s = sb("bn_s", [D, 4])
        dst_rel = sb("dst_rel", [P, CHUNKS, TILES])
        chunk_ends = sb("chunk_ends", [P, 2, CHUNKS])
        ends_col = sb("ends_col", [BLOCK, 2, SLOTS])
        ends_diag = sb("ends_diag", [BLOCK, 2, SLOTS, BLOCK])
        ends_row = sb("ends_row", [P, 2, CHUNKS])
        base_i = sb("base_i", [1, CHUNKS], I32)
        span = sb("span", [1, CHUNKS])
        span_max = sb("span_max", [1, 1])
        further = sb("further", [1, FURTHER])
        further_n = sb("further_n", [1, 1])
        further_i = sb("further_i", [1, 1], I32)
        src_s = [sb(f"src_s{q}", [P, TILES], I32) for q in range(2 * SLOTS)]
        attr_s = [sb(f"attr_s{j}", [P, TILES, FEAT]) for j in range(SLOTS)]
        h_src = [sb(f"h_src{j}", [P, TILES, D]) for j in range(SLOTS)]
        h_parts = [sb(f"h_parts{j}", [P, TILES, 2, D], F32R) for j in range(SLOTS)]
        prods = sb("prods", [P, SLOTS, TILES * FD])
        prod = [prods[:, j, :].rearrange("p (t f i) -> p t f i", t=TILES, f=FEAT) for j in range(SLOTS)]
        dst_i = prods[:].rearrange("p j n -> p (j n)")[:, 0:CHUNKS * TILES].bitcast(I32) \
            .rearrange("p (c t) -> p c t", t=TILES)
        onehot = [sb(f"onehot{j}", [P, TILES, WINDOW], F32R) for j in range(SLOTS)]
        g_feat = [sb(f"g_feat{j}", [FD, WINDOW]) for j in range(SLOTS)]
        g_bias = [sb(f"g_bias{j}", [2 * D, WINDOW]) for j in range(SLOTS)]
        src_i = sb("src_i", [BLOCK, CROWS, PICKED * P], I32)
        code = sb("code", [BLOCK, CROWS, PICKED * P], F16)
        cols_i = sb("cols_i", [P, CHUNKS, PICKED], I32)
        rest = sb("rest", [P, CHUNKS, PICKED])
        rowpart_i = sb("rowpart_i", [P, PARTS], I32)
        rowpart = sb("rowpart", [P, PARTS], F16)
        rowpart_neg = sb("rowpart_neg", [P, PARTS])
        h_split = sb("h_split", [ROWS, SPLITS, PARTS, PART * D], F32R)
        h_left = sb("h_left", [ROWS, COLS, D])
        ln_sq = h_left
        code_s = [sb(f"code_s{j}", [ROWS, PICKED, P], F16) for j in range(SLOTS)]
        pick_hots = sb("pick_hots", [P, SLOTS, PICKED * PARTS * P], F32R)
        pick_hot = [pick_hots[0:ROWS, j, :].rearrange("b (k m e) -> b k m e", k=PICKED, m=PARTS)
                    for j in range(SLOTS)]
        picked = [sb(f"picked{k}", [P, D, PART]) for k in range(3)]
        wide_hot = pick_hots[:].rearrange("p j n -> p (j n)")[:, 0:TILES * WIDE] \
            .rearrange("p (t w) -> p t w", t=TILES)
        wide_feat = sb("wide_feat", [FD, WIDE])
        wide_bias = sb("wide_bias", [2 * D, WIDE])

        ps_g = ctx.enter_context(nc.psum_tensor("ps_g", [P, SLOTS, 512], F32))
        ps_p = ctx.enter_context(nc.psum_tensor("ps_p", [P, 3, 512], F32))
        ps_n = ps_p
        G_FEAT, G_BIAS, G_OUT = (slice(k * WINDOW, (k + 1) * WINDOW) for k in range(3))

        s_rowsrc = sem("s_rowsrc")
        s_code_steps = sem("s_code_steps")
        s_code = sem("s_code")
        s_code_out = sem("s_code_out")
        s_codes = [sem(f"s_codes{j}") for j in range(SLOTS)]
        s_split = sem("s_split")
        s_far = sem("s_far")
        s_hot = sem("s_hot")
        s_more = sem("s_more")
        s_pick = sem("s_pick")
        s_masked = sem("s_masked")
        s_picked = sem("s_picked")
        s_weights = sem("s_weights")
        s_x = sem("s_x")
        s_dst = sem("s_dst")
        s_const = sem("s_const")
        s_iota = sem("s_iota")
        s_ln = sem("s_ln")
        s_ln_std = sem("s_ln_std")
        s_prep = sem("s_prep")
        s_ends_t = sem("s_ends_t")
        s_ends_b = sem("s_ends_b")
        s_bases = sem("s_bases")
        s_table = sem("s_table")
        s_rows = sem("s_rows")
        s_turn = sem("s_turn")
        s_turned = sem("s_turned")
        s_src = [sem(f"s_src{q}") for q in range(2 * SLOTS)]
        s_attr = [sem(f"s_attr{j}") for j in range(SLOTS)]
        s_gath = [sem(f"s_gath{j}") for j in range(SLOTS)]
        s_form = sem("s_form")
        s_high = sem("s_high")
        s_dist = sem("s_dist")
        s_onehot = sem("s_onehot")
        s_g = sem("s_g")
        s_gcopy = sem("s_gcopy")
        s_agg = sem("s_agg")
        s_add = sem("s_add")
        s_bn = sem("s_bn")
        s_bn_std = sem("s_bn_std")
        s_bn_done = sem("s_bn_done")
        s_relu = sem("s_relu")
        s_out = sem("s_out")
        s_fin = sem("s_fin")
        w_src, w_attr, w_gath, w_rows = sem("w_src"), sem("w_attr"), sem("w_gath"), sem("w_rows")
        w_go_sp, w_form, w_g, w_copy, w_agg = (sem("w_go_sp"), sem("w_form"), sem("w_g"),
                                                sem("w_copy"), sem("w_agg"))
        w_go_pool, w_iota, w_high, w_add = sem("w_go_pool"), sem("w_iota"), sem("w_high"), sem("w_add")
        s_start = sem("s_start")
        s_whole = sem("s_whole")

        rows_of = lambda t: t.rearrange("(p j) d -> p j d", j=COLS)
        by_col = nodes[:, 0:N].rearrange("q (p j) -> q j p", j=COLS)
        by_row = nodes[:, 0:N].rearrange("q (p j) -> q p j", j=COLS)

        TURNS_IN = COLS // PER_T
        TURNS_OUT = COLS // PER_R
        ROOTS = [NBLOCKS - 2 * (NBLOCKS // 3), NBLOCKS - NBLOCKS // 3, NBLOCKS]

        def turns_before(layer):
            return TURNS_IN + layer * (NBLOCKS + TURNS_OUT)

        def further_windows(eng, engine_type, body):
            n = nc.values_load(further_i[0:1, 0:1], engines=(engine_type,), min_val=0,
                               max_val=FURTHER,
                               skip_runtime_bounds_check_because="a sum of FURTHER zeros or ones")
            with eng.If(n > 0):
                with eng.Fori(0, n) as w:
                    body.window(w)
                    with eng.Fori(0, CHUNKS) as c:
                        body.chunk(w, c)
            with eng.Else():
                eng.nop()

        class Body:
            def __init__(self, window, chunk):
                self.window, self.chunk = window, chunk

        def taken(eng, s, n):
            eng.wait_ge(s, n)
            eng.sem_clear(s)

        def ends_bank(m, k):
            n = m * SLOTS + k
            return ps_g[:, n // 4, n % 4 * P:(n % 4 + 1) * P]

        def root_bank(b):
            return ps_g[0:D, SLOTS - 2 + b % 2, 0:NB]

        def unit_bank(u):
            same = [k for k in range(UNITS) if k % 3 == u % 3]
            n = same.index(u)
            return u % 3, (u - same[n - 1] if n else u - same[-1] + UNITS)

        def rounds(eng, step, roots=None):
            for j in range(SLOTS):
                step(0, j, True, False)
                if roots and j + 1 < len(ROOTS):
                    roots(ROOTS[j], ROOTS[j + 1])
            with eng.Fori(1, ROUNDS - 1) as r:
                for j in range(SLOTS):
                    step(r, j, False, False)
            for j in range(SLOTS):
                step(ROUNDS - 1, j, False, True)

        def pairs(eng, start, end, step):
            if start % 2 == 0:
                step(start, start // 2, 0)
                start += 1
            n = (end - start) // 2
            if n:
                with eng.Fori(start // 2, start // 2 + n) as p:
                    step(2 * p + 1, p, 1)
                    step(2 * p + 2, p + 1, 0)
            if (end - start) % 2:
                step(end - 1, (end - 1) // 2, 1)

        def src_loaded(half, odd, layer):
            uses = (ROUNDS + 1 - odd) // 2
            return (half + 1 + layer * uses) * 16

        def ahead(r, j, last, n):
            if j + n < SLOTS:
                return r, j + n
            return None if last else (r + 1, j + n - SLOTS)

        block = ctx.enter_context(nc.Block())

        @block.sync
        def _(sp):
            def first_loads():
                for q in range(2 * SLOTS):
                    sp.dma_start(src_s[q][:], src[q]).then_inc(s_src[q], 16)
                for j in range(SLOTS):
                    sp.dma_start(attr_s[j][:], edge_attr[j].rearrange("p (t f) -> p t f", t=TILES)) \
                      .then_inc(s_attr[j], 16)

            sp.dma_start(x_rows[:], rows_of(x)).then_inc(s_x, 16)
            first_loads()
            sp.dma_start(dst_i, dst).then_inc(s_dst, 16)
            for tile, view in (
                (w_feat[:], edge_w.rearrange("l f (i o) -> (f i) l o", o=D)),
                (w_bias[0:D], edge_b.rearrange("l (i o) -> i l o", o=D)),
                (w_bias[D:2 * D], edge_b.rearrange("l (i o) -> i l o", o=D)),
                (w_root[:], root_w.rearrange("l i o -> i l o")),
                (b_root[:], root_bt), (gamma[:], gamma_t), (beta[:], beta_t),
                (w_pred[:], pred_w), (b_pred[:], pred_b.to_broadcast([ROWS, D])),
            ):
                sp.dma_start(tile, view).then_inc(s_weights, 16)

            sp.dma_start(src_i[:], src_rows.rearrange("(b c) e -> b c e", c=CROWS)).then_inc(s_rowsrc, 16)
            sp.dma_start(cols_i[:], src_cols).then_inc(s_rowsrc, 16)

            def load_codes(c, j):
                n = PICKS[j] * P
                if n:
                    sp.dma_start(code_s[j][:, 0:PICKS[j], :].rearrange("b k e -> b (k e)"),
                                 code_table[c, 0:n].to_broadcast([ROWS, n])).then_inc(s_codes[j], 16)

            for layer in range(LAYERS):
                done = layer * CHUNKS
                sp.wait_ge(s_rows, layer + 1 if layer == 0 else 1 + layer * TURNS_OUT)
                sp.dma_start(rows_of(h_table), h_rows[:]).then_inc(s_table, 16)
                if layer == 0:
                    sp.wait_ge(s_code, 1)
                    sp.dma_start(code_table.rearrange("(b c) e -> b c e", c=CROWS), code[:]).then_inc(s_code_out, 16)
                    sp.wait_ge(s_code_out, 16)
                for c in range(SLOTS):
                    load_codes(slice(c, c + 1), c)
                def codes_used(r, j):
                    sp.wait_ge(s_hot, r * SLOTS + j + 1 + done)
                    sp.sem_inc(s_start, 1)
                    if MORE[j]:
                        sp.wait_ge(s_more, more(r, j, layer))
                        sp.sem_inc(s_start, 1)

                for c in range(SLOTS, SLOTS + 2):
                    codes_used(0, c - SLOTS)
                    load_codes(slice(c, c + 1), c - SLOTS)

                def step(r, j, odd, last):
                    c = r * SLOTS + j
                    sp.wait_ge(s_form, c - SLOTS + 1 + done)
                    if not last:
                        q = (1 - odd) * SLOTS + j
                        sp.dma_start(src_s[q][:], src[bass.ds(c + SLOTS, 1)].rearrange("a p t -> (a p) t")) \
                          .then_inc(s_src[q], 16)
                    sp.dma_start(attr_s[j][:], edge_attr[bass.ds(c, 1)].rearrange("a p (t f) -> (a p) t f", t=TILES)) \
                      .then_inc(s_attr[j], 16)
                    if then := ahead(r, j, last, 2):
                        codes_used(then[0] - 1, then[1])
                        load_codes(bass.ds(c + 2, 1), then[1])

                def one_round(r, half, odd):
                    for j in range(SLOTS):
                        step(r, j, odd, False)

                pairs(sp, 1, ROUNDS - 1, one_round)
                for j in range(SLOTS):
                    step(ROUNDS - 1, j, (ROUNDS - 1) % 2, True)

                def window(w):
                    pass

                def chunk(w, c):
                    taken(sp, w_go_sp, 1)
                    sp.dma_start(src_s[0][:], src[bass.ds(c, 1)].rearrange("a p t -> (a p) t")).then_inc(w_src, 16)
                    sp.dma_start(attr_s[0][:], edge_attr[bass.ds(c, 1)].rearrange("a p (t f) -> (a p) t f", t=TILES)).then_inc(w_attr, 16)

                sp.wait_ge(s_bases, 1)
                sp.wait_ge(s_form, done + CHUNKS)
                further_windows(sp, mybir.EngineType.SP, Body(window, chunk))
                if layer < LAYERS - 1:
                    sp.wait_ge(s_whole, layer + 1)
                    first_loads()

            sp.wait_ge(s_fin, 2 * TURNS_OUT)
            sp.dma_start(rows_of(out), h_rows[:]).then_inc(s_out, 16)
            sp.wait_ge(s_out, 16)

        @block.gpsimd
        def _(pool):
            pool.memset(ident[:], 0.0).then_inc(s_const, 1)
            pool.memset(ones[:], 1.0).then_inc(s_const, 1)
            pool.iota(iota_i[:], pattern=[[1, WIDE]], base=0, channel_multiplier=0).then_inc(s_const, 1)
            pool.iota(rowpart_i[:], pattern=[[1, PARTS]], base=0, channel_multiplier=PARTS).then_inc(s_const, 1)
            pool.wait_ge(s_const, 4)
            pool.affine_select(out=ident[:], in_=ident[:], compare_op=ALU.not_equal, fill=1.0,
                               base=0, pattern=[[-1, P]], channel_multiplier=1).then_inc(s_const, 1)

            def gather(j, q, signal, first_tile):
                for t in range(first_tile, TILES):
                    pool.indirect_dma_start(
                        out=h_src[j][:, t, :], out_offset=None, in_=h_table,
                        in_offset=bass.IndirectOffsetOnAxis(ap=src_s[q][:, t:t + 1], axis=0)
                    ).then_inc(signal, 16)

            for layer in range(LAYERS):
                done = layer * CHUNKS
                pool.wait_ge(s_table, 16 * (layer + 1))

                def one_round(r, half, odd):
                    for j in range(SLOTS):
                        q = odd * SLOTS + j
                        pool.wait_ge(s_src[q], src_loaded(half, odd, layer))
                        pool.sem_inc(s_start, 1)
                        if not isinstance(r, int) or r > 0:
                            pool.wait_ge(s_form, (r - 1) * SLOTS + j + 1 + done)
                            pool.sem_inc(s_start, 1)
                        gather(j, q, s_gath[j], PICKS[j])

                pairs(pool, 0, ROUNDS, one_round)

                def chunk(w, c):
                    taken(pool, w_go_pool, 1)
                    taken(pool, w_src, 16)
                    gather(0, 0, w_gath, 0)
                    pool.wait_ge(w_gath, 16 * TILES)
                    pool.dma_reset(range(w_gath.num, w_gath.num + 1))
                    pool.sem_clear(w_gath)
                    pool.sem_inc(w_rows, 1)

                pool.wait_ge(s_bases, 1)
                pool.wait_ge(s_g, done + CHUNKS)
                further_windows(pool, mybir.EngineType.Pool, Body(lambda w: None, chunk))

        @block.tensor
        def _(pe):
            mm = nc.tensor.matmul
            pe.wait_ge(s_const, 5)
            pe.wait_ge(s_rows, 1)
            for k in range(TURNS_IN):
                if k >= 2:
                    pe.wait_ge(s_turned, k - 1)
                for q in range(PER_T):
                    last = nc.tensor.transpose(ps_n[0:D, k % 2, q * ROWS:(q + 1) * ROWS],
                                               h_rows[:, k * PER_T + q, :], ident[0:ROWS, 0:ROWS])
                last.then_inc(s_turn, 1)
            pe.wait_ge(s_prep, 3)
            for k in range(SLOTS):
                for m in range(2):
                    last = nc.tensor.transpose(ends_bank(m, k)[0:BLOCK, :],
                                               chunk_ends[:, m, k * BLOCK:(k + 1) * BLOCK], ident[:])
            last.then_inc(s_ends_t, 1)
            pe.wait_ge(s_prep, 6)
            for k in range(SLOTS):
                for m in range(2):
                    last = mm(ends_bank(m, k)[:, 0:BLOCK], ones[0:BLOCK, :],
                              ends_diag[:, m, k, :], start=True, stop=True)
            last.then_inc(s_ends_b, 1)
            pe.wait_ge(s_weights, 9 * 16)

            def reduce_chunk(feat, bias, h, z, hot):
                for t in range(TILES):
                    mm(feat, z[:, t, :, :].rearrange("p f i -> p (f i)"), hot[:, t, :].bitcast(F32),
                       start=(t == 0), stop=(t == TILES - 1))
                for t in range(TILES):
                    last = mm(bias, h[:, t, :, :].rearrange("p s i -> p (s i)"), hot[:, t, :],
                              start=(t == 0), stop=(t == TILES - 1))
                return last

            def apply_w(layer, to, feat, bias):
                mm(to, w_feat[:, layer, :], feat, start=True, stop=False)
                return mm(to, w_bias[:, layer, :], bias, start=False, stop=True)

            for layer in range(LAYERS):
                done = layer * CHUNKS
                before = turns_before(layer)

                def roots(start, end):
                    for b in range(start, end):
                        pe.wait_ge(s_turned, before + max(b - 1, 0))
                        mm(root_bank(b), w_root[:, layer, :], nodes[:, b * NB:(b + 1) * NB],
                           start=True, stop=True).then_inc(s_turn, 1)

                roots(0, ROOTS[0])
                if layer == 0:
                    pe.wait_ge(s_bases, 1)

                def pick_step(r, j, first):
                    c = r * SLOTS + j
                    pe.wait_ge(s_hot, c + 1 + done)
                    if MORE[j]:
                        pe.wait_ge(s_more, more(r, j, layer))
                    for k in range(PICKS[j]):
                        u = FIRST_UNIT[j] + k
                        bank, before_it = unit_bank(u)
                        if not (first and u < before_it):
                            pe.wait_ge(s_masked, r * UNITS + u + 1 - before_it + layer * ROUNDS * UNITS)
                        for m in range(PARTS):
                            for h in range(SPLITS):
                                last = mm(ps_p[:, bank, 0:PART * D], pick_hot[j][:, k, m, :], h_split[:, h, m, :],
                                          start=(m == 0 and h == 0), stop=(m == PARTS - 1 and h == SPLITS - 1))
                        last.then_inc(s_pick, 1)

                def reduce_step(r, j, first):
                    c = r * SLOTS + j
                    pe.wait_ge(s_onehot, c + 1 + done)
                    pe.wait_ge(s_form, c + 1 + done)
                    if first and j == SLOTS - 2:
                        pe.wait_ge(s_turned, before + NBLOCKS)
                    if not (first and layer == 0):
                        pe.wait_ge(s_add, c - SLOTS + 1 + done)
                    reduce_chunk(ps_g[:, j, G_FEAT], ps_g[0:2 * D, j, G_BIAS],
                                 h_parts[j], prod[j], onehot[j]).then_inc(s_g, 1)

                def apply_step(r, j, first):
                    c = r * SLOTS + j
                    pe.wait_ge(s_gcopy, (c + 1 + done) * 2)
                    apply_w(layer, ps_g[0:D, j, G_OUT], g_feat[j][:],
                            g_bias[j][:]).then_inc(s_agg, 1)

                def step(r, j, first, last):
                    if then := ahead(r, j, last, 2):
                        pick_step(*then, first and j + 2 < SLOTS)
                    reduce_step(r, j, first)
                    if j:
                        apply_step(r, j - 1, first)
                    elif not first:
                        apply_step(r - 1, SLOTS - 1, False)

                pe.wait_ge(s_split, SPLIT_STEPS * (layer + 1))
                pe.wait_ge(s_turned, before)
                pick_step(0, 0, True)
                pick_step(0, 1, True)
                rounds(pe, step, roots)
                apply_step(ROUNDS - 1, SLOTS - 1, False)

                def chunk(w, c):
                    taken(pe, w_form, 2)
                    reduce_chunk(ps_g[:, 0, :], ps_g[0:2 * D, 1, :], h_parts[0], prod[0], wide_hot).then_inc(w_g, 1)
                    taken(pe, w_copy, 2)
                    apply_w(layer, ps_g[0:D, 2, :], wide_feat[:], wide_bias[:]).then_inc(w_agg, 1)

                pe.wait_ge(s_gcopy, 2 * (done + CHUNKS))
                pe.wait_ge(s_add, done + CHUNKS)
                further_windows(pe, mybir.EngineType.PE, Body(lambda w: None, chunk))

                if layer < LAYERS - 1:
                    for k in range(TURNS_OUT):
                        n = before + NBLOCKS + k
                        pe.wait_ge(s_relu, layer * TURNS_OUT + k + 1)
                        pe.wait_ge(s_turned, n - 1)
                        for q in range(PER_R):
                            last = nc.tensor.transpose(ps_n[0:ROWS, n % 2, q * D:(q + 1) * D],
                                                       by_col[:, k * PER_R + q, :], ident[0:D, 0:D])
                        last.then_inc(s_turn, 1)
                else:
                    for k in range(TURNS_OUT):
                        n = before + NBLOCKS + k
                        pe.wait_ge(s_relu, layer * TURNS_OUT + k + 1)
                        if k >= 2:
                            pe.wait_ge(s_fin, 2 * (k - 1))
                        else:
                            pe.wait_ge(s_turned, n - k)
                        for q in range(PER_R):
                            last = mm(ps_n[0:ROWS, n % 2, q * D:(q + 1) * D],
                                      by_col[:, k * PER_R + q, :], w_pred[:], start=True, stop=True)
                        last.then_inc(s_turn, 1)

        @block.scalar
        def _(act):
            copy = lambda o, i: nc.scalar.activation(o, i, ACT.Copy)
            act.wait_ge(s_ln, 6)
            nc.scalar.activation(ln_b[:], ln_a[:], ACT.Sqrt).then_inc(s_ln_std, 1)
            for k in range(TURNS_IN):
                act.wait_ge(s_turn, k + 1)
                copy(by_col[:, k * PER_T:(k + 1) * PER_T, :],
                     ps_n[0:D, k % 2, 0:NB].rearrange("q (j p) -> q j p", p=ROWS)).then_inc(s_turned, 1)
            act.wait_ge(s_weights, 9 * 16)

            for layer in range(LAYERS):
                done = layer * CHUNKS
                before = turns_before(layer)

                def roots(start, end):
                    for b in range(start, end):
                        act.wait_ge(s_turn, before + b + 1)
                        nc.scalar.activation(nodes[:, b * NB:(b + 1) * NB], root_bank(b),
                                             ACT.Identity, bias=b_root[:, layer:layer + 1]).then_inc(s_turned, 1)

                def far_step(r, j, first):
                    if not MORE[j]:
                        return
                    act.wait_ge(s_codes[j], (r + 1 + layer * ROUNDS) * 16)
                    if not (first and layer == 0):
                        act.wait_ge(s_pick, (r - 1 + layer * ROUNDS) * UNITS + FIRST_UNIT[j] + PICKS[j])
                    for m in range(PARTS):
                        last = nc.scalar.activation(pick_hot[j][:, 1, m, :], code_s[j][:, 1, :], ACT.Abs,
                                                    bias=rowpart_neg[0:ROWS, m:m + 1])
                    last.then_inc(s_far, 1)

                def hot_step(r, j):
                    if not MORE[j]:
                        return
                    act.wait_ge(s_far, more(r, j, layer))
                    nc.scalar.activation(pick_hot[j][:, 1], pick_hot[j][:, 1], ACT.Relu, scale=-1.0,
                                         bias=1.0).then_inc(s_more, 1)

                def dist_step(r, j, first):
                    if not (first and layer == 0):
                        act.wait_ge(s_g, r * SLOTS + j - SLOTS + 1 + done)
                    for t in range(TILES):
                        last = nc.scalar.activation(onehot[j][:, t, :], iota[:, 0:WINDOW], ACT.Abs, scale=-1.0,
                                                    bias=dst_rel[:, bass.ds(r * SLOTS + j, 1), t])
                    last.then_inc(s_dist, 1)

                def onehot_step(r, j):
                    act.wait_ge(s_dist, r * SLOTS + j + 1 + done)
                    nc.scalar.activation(onehot[j][:], onehot[j][:], ACT.Relu, scale=-1.0, bias=1.0) \
                        .then_inc(s_onehot, 1)

                def copy_step(r, j, first):
                    c = r * SLOTS + j
                    act.wait_ge(s_g, c + 1 + done)
                    if not (first and layer == 0):
                        act.wait_ge(s_agg, c - SLOTS + 1 + done)
                    copy(g_feat[j][:], ps_g[:, j, G_FEAT]).then_inc(s_gcopy, 1)
                    copy(g_bias[j][:], ps_g[0:2 * D, j, G_BIAS]).then_inc(s_gcopy, 1)

                def step(r, j, first, last):
                    later, then = ahead(r, j, last, 4), ahead(r, j, last, 2)
                    if later:
                        far_step(*later, first and j + 4 < SLOTS)
                    if then:
                        dist_step(*then, first and j + 2 < SLOTS)
                    if later:
                        hot_step(*later)
                    if then:
                        onehot_step(*then)
                    copy_step(r, j, first)

                roots(0, ROOTS[0])
                act.wait_ge(s_code_steps, 6)
                act.wait_ge(s_bases, 1)
                for j in range(4):
                    far_step(0, j, True)
                    hot_step(0, j)
                for j in range(2):
                    dist_step(0, j, True)
                    onehot_step(0, j)
                rounds(act, step, roots)

                def chunk(w, c):
                    taken(act, w_g, 1)
                    copy(wide_feat[:], ps_g[:, 0, :]).then_inc(w_copy, 1)
                    copy(wide_bias[:], ps_g[0:2 * D, 1, :]).then_inc(w_copy, 1)

                further_windows(act, mybir.EngineType.Activation, Body(lambda w: None, chunk))

                if layer < LAYERS - 1:
                    act.wait_ge(s_bn, (layer + 1) * (NBLOCKS + 2))
                    nc.scalar.activation(bn_s[:, 1:2], bn_s[:, 0:1], ACT.Sqrt).then_inc(s_bn_std, 1)
                    act.wait_ge(s_bn_done, 4 * (layer + 1))
                else:
                    act.wait_ge(s_whole, LAYERS)
                scale = bn_s[:, 2:3] if layer < LAYERS - 1 else 1.0
                shift = bn_s[:, 3:4] if layer < LAYERS - 1 else 0.0

                def relu(k):
                    part = by_row[:, :, k * PER_R:(k + 1) * PER_R]
                    nc.scalar.activation(part, part, ACT.Relu, bias=shift, scale=scale).then_inc(s_relu, 1)

                relu(0)
                for k in range(TURNS_OUT):
                    if k + 1 < TURNS_OUT:
                        relu(k + 1)
                    if layer < LAYERS - 1:
                        n = before + NBLOCKS + k
                        act.wait_ge(s_turn, n + 1)
                        if k == 0:
                            act.wait_ge(s_table, 16 * (layer + 1))
                        copy(h_rows[:, k * PER_R:(k + 1) * PER_R, :].rearrange("p j d -> p (j d)"),
                             ps_n[0:ROWS, n % 2, 0:PER_R * D]).then_inc(s_turned, 1)
                        act.wait_ge(s_turned, n + 1)
                        act.sem_inc(s_rows, 1)

        @block.vector
        def _(dve):
            v = nc.vector
            dve.wait_ge(s_x, 16)
            wide = lambda t: t[:].unsqueeze(2).to_broadcast([ROWS, COLS, D])
            v.tensor_reduce(ln_a[:], x_rows[:], AX.X, ALU.add).then_inc(s_ln, 1)
            dve.wait_ge(s_ln, 1)
            v.tensor_scalar(ln_b[:], ln_a[:], 1.0 / D, None, ALU.mult).then_inc(s_ln, 1)
            dve.wait_ge(s_ln, 2)
            v.tensor_tensor(h_rows[:], x_rows[:], wide(ln_b), ALU.subtract).then_inc(s_ln, 1)
            dve.wait_ge(s_ln, 3)
            squares = ln_sq[:]
            v.tensor_tensor(squares, h_rows[:], h_rows[:], ALU.mult).then_inc(s_ln, 1)
            dve.wait_ge(s_ln, 4)
            v.tensor_reduce(ln_b[:], squares, AX.X, ALU.add).then_inc(s_ln, 1)
            dve.wait_ge(s_ln, 5)
            v.tensor_scalar(ln_a[:], ln_b[:], 1.0 / D, LN_EPS, ALU.mult, ALU.add).then_inc(s_ln, 1)
            dve.wait_ge(s_ln_std, 1)
            v.reciprocal(ln_a[:], ln_b[:]).then_inc(s_ln, 1)
            dve.wait_ge(s_ln, 7)
            v.tensor_tensor(h_rows[:], h_rows[:], wide(ln_a), ALU.mult).then_inc(s_ln, 1)
            dve.wait_ge(s_ln, 8)
            v.tensor_scalar(h_rows[:], h_rows[:], 0.0, None, ALU.max).then_inc(s_rows, 1)

            by_part = (1.0 / PART, -(PART - 1) / (2.0 * PART), ALU.mult, ALU.add)
            code_f = ln_sq[0:BLOCK].rearrange("b j d -> b (j d)")[:, 0:CROWS * PICKED * P]
            flat = lambda t: t[:].rearrange("b c e -> b (c e)")
            dve.wait_ge(s_rowsrc, 32)
            v.tensor_scalar(code_f, flat(src_i), *by_part).then_inc(s_code_steps, 1)
            dve.wait_ge(s_code_steps, 1)
            v.tensor_scalar(flat(code), code_f, ROUND, -ROUND, ALU.add, ALU.add).then_inc(s_code, 1)
            v.tensor_scalar(rest[:], cols_i[:], *by_part).then_inc(s_code_steps, 1)
            dve.wait_ge(s_code_steps, 2)
            v.tensor_scalar(rest[:], rest[:], ROUND, -ROUND, ALU.add, ALU.add).then_inc(s_code_steps, 1)
            dve.wait_ge(s_code_steps, 3)
            v.scalar_tensor_tensor(rest[:], rest[:], -float(PART), cols_i[:], ALU.mult, ALU.add).then_inc(s_code_steps, 1)

            dve.wait_ge(s_const, 5)
            v.tensor_copy(iota[:], iota_i[:]).then_inc(s_iota, 1)
            v.tensor_copy(rowpart[:], rowpart_i[:]).then_inc(s_code_steps, 1)
            v.tensor_scalar(rowpart_neg[:], rowpart_i[:], -1.0, None, ALU.mult).then_inc(s_code_steps, 1)
            v.memset(nodes[:, N:N + WIDE], 0.0)
            dve.wait_ge(s_dst, 16)
            v.tensor_copy(dst_rel[:], dst_i).then_inc(s_prep, 1)
            dve.wait_ge(s_prep, 1)
            v.tensor_reduce(chunk_ends[:, 0, :], dst_rel[:], AX.X, ALU.min).then_inc(s_prep, 1)
            v.tensor_reduce(chunk_ends[:, 1, :], dst_rel[:], AX.X, ALU.max).then_inc(s_prep, 1)
            dve.wait_ge(s_ends_t, 1)
            for m, op in enumerate((ALU.min, ALU.max)):
                for k in range(SLOTS):
                    last = v.tensor_reduce(ends_col[:, m, k:k + 1], ends_bank(m, k)[0:BLOCK, :], AX.X, op)
                last.then_inc(s_prep, 1)
            dve.wait_ge(s_prep, 5)
            v.tensor_tensor(
                ends_diag[:].rearrange("p m k c -> p (m k) c"),
                ends_col[:].rearrange("p m k -> p (m k)").unsqueeze(2).to_broadcast([BLOCK, 2 * SLOTS, BLOCK]),
                ident[0:BLOCK, 0:BLOCK].unsqueeze(1).to_broadcast([BLOCK, 2 * SLOTS, BLOCK]),
                ALU.mult).then_inc(s_prep, 1)
            dve.wait_ge(s_ends_b, 1)
            for m in range(2):
                for k in range(SLOTS):
                    last = v.tensor_copy(ends_row[:, m, k * BLOCK:(k + 1) * BLOCK], ends_bank(m, k)[:, 0:BLOCK])
                last.then_inc(s_prep, 1)
            dve.wait_ge(s_prep, 8)
            v.tensor_tensor(dst_rel[:], dst_rel[:], ends_row[:, 0, :].unsqueeze(2).to_broadcast([P, CHUNKS, TILES]),
                            ALU.subtract).then_inc(s_prep, 1)
            v.tensor_copy(base_i[:], ends_row[0:1, 0, :]).then_inc(s_prep, 1)
            v.tensor_tensor(span[:], ends_row[0:1, 1, :], ends_row[0:1, 0, :], ALU.subtract).then_inc(s_prep, 1)
            dve.wait_ge(s_prep, 11)
            dve.wait_ge(s_iota, 1)
            v.tensor_reduce(span_max[:], span[:], AX.X, ALU.max).then_inc(s_prep, 1)
            v.tensor_scalar(further[:], iota[0:1, 0:FURTHER], float(WIDE), float(WINDOW), ALU.mult, ALU.add) \
                .then_inc(s_prep, 1)
            dve.wait_ge(s_prep, 13)
            v.tensor_scalar(further[:], further[:], span_max[:], None, ALU.is_le).then_inc(s_prep, 1)
            dve.wait_ge(s_prep, 14)
            v.tensor_reduce(further_n[:], further[:], AX.X, ALU.add).then_inc(s_prep, 1)
            dve.wait_ge(s_prep, 15)
            v.tensor_copy(further_i[:], further_n[:]).then_inc(s_bases, 1)
            dve.wait_ge(s_bases, 1)

            def products(j):
                return v.tensor_tensor(
                    prod[j],
                    attr_s[j][:].unsqueeze(3).to_broadcast([P, TILES, FEAT, D]),
                    h_src[j][:].unsqueeze(2).to_broadcast([P, TILES, FEAT, D]), ALU.mult)

            def lower_part(j):
                return v.tensor_tensor(h_parts[j][:, :, 1, :], h_src[j][:], h_parts[j][:, :, 0, :], ALU.subtract)

            def one_hots(hot, c, row, width):
                return v.tensor_tensor(
                    hot, dst_rel[:, bass.ds(c, 1), :].rearrange("p a t -> p (a t)").unsqueeze(2).to_broadcast([P, TILES, width]),
                    row.unsqueeze(1).to_broadcast([P, TILES, width]), ALU.is_equal)

            for layer in range(LAYERS):
                done = layer * CHUNKS

                dve.wait_ge(s_rows, 1 + layer * TURNS_OUT)
                left, n_split = h_rows, SPLIT_STEPS * layer
                for h in range(SPLITS):
                    part = h_split[:, h, :, :].rearrange("b m c -> b (m c)")
                    whole = left[:].rearrange("b j d -> b (j d)")
                    v.tensor_copy(part, whole).then_inc(s_split, 1)
                    n_split += 1
                    dve.wait_ge(s_split, n_split)
                    if h < SPLITS - 1:
                        v.tensor_tensor(h_left[:].rearrange("b j d -> b (j d)"), whole, part, ALU.subtract) \
                            .then_inc(s_split, 1)
                        n_split += 1
                        dve.wait_ge(s_split, n_split)
                    left = h_left

                def hot_step(r, j, first):
                    dve.wait_ge(s_codes[j], (r + 1 + layer * ROUNDS) * 16)
                    if not (first and layer == 0):
                        dve.wait_ge(s_pick, (r - 1 + layer * ROUNDS) * UNITS + FIRST_UNIT[j] + PICKS[j])
                    v.tensor_tensor(
                        pick_hot[j][:, 0], code_s[j][:, 0:1, :].to_broadcast([ROWS, PARTS, P]),
                        rowpart[0:ROWS, :].unsqueeze(2).to_broadcast([ROWS, PARTS, P]),
                        ALU.is_equal).then_inc(s_hot, 1)

                def mask_step(r, j, first, tiles):
                    c = r * SLOTS + j
                    for k in tiles:
                        u = FIRST_UNIT[j] + k
                        n = r * UNITS + u + layer * ROUNDS * UNITS
                        bank, before_it = unit_bank(u)
                        dve.wait_ge(s_pick, n + 1)
                        if not (first and u < before_it):
                            dve.wait_ge(s_picked, n + 1 - before_it)
                        to = picked[bank]
                        v.scalar_tensor_tensor(
                            to[:], iota[:, 0:PART].unsqueeze(1).to_broadcast([P, D, PART]),
                            rest[:, bass.ds(c, 1), k],
                            ps_p[:, bank, 0:PART * D].rearrange("p (s d) -> p d s", d=D),
                            ALU.is_equal, ALU.mult).then_inc(s_masked, 1)

                def picked_step(r, j):
                    for k in range(PICKS[j]):
                        u = FIRST_UNIT[j] + k
                        dve.wait_ge(s_masked, r * UNITS + u + 1 + layer * ROUNDS * UNITS)
                        v.tensor_reduce(h_src[j][:, k, :], picked[unit_bank(u)[0]][:], AX.X, ALU.add) \
                            .then_inc(s_picked, 1)

                def upper_step(r, j, first):
                    c = r * SLOTS + j
                    if not (first and layer == 0):
                        dve.wait_ge(s_g, c - SLOTS + 1 + done)
                    dve.wait_ge(s_gath[j], (r + 1 + layer * ROUNDS) * 16 * (TILES - PICKS[j]))
                    dve.wait_ge(s_picked, (r + layer * ROUNDS) * UNITS + FIRST_UNIT[j] + PICKS[j])
                    v.tensor_copy(h_parts[j][:, :, 0, :], h_src[j][:]).then_inc(s_high, 1)

                def form_step(r, j, first):
                    c = r * SLOTS + j
                    dve.wait_ge(s_attr[j], (r + 1 + layer * ROUNDS) * 16)
                    products(j)
                    dve.wait_ge(s_high, c + 1 + done)
                    lower_part(j).then_inc(s_form, 1)

                def add_step(r, j, first, base):
                    c = r * SLOTS + j
                    dve.wait_ge(s_agg, c + 1 + done)
                    if not (first and layer == 0 and j == 0):
                        dve.wait_ge(s_add, c + done)
                    at = nodes[:, bass.ds(base, WINDOW)]
                    v.tensor_tensor(at, at, ps_g[0:D, j, G_OUT], ALU.add).then_inc(s_add, 1)

                def base_of(c):
                    return nc.values_load(base_i[0:1, bass.ds(c, 1)], engines=(DVE,), min_val=0,
                                          max_val=N, skip_runtime_bounds_check_because="a node's number")

                def step(r, j, first, last):
                    if then := ahead(r, j, last, 3):
                        hot_step(*then, first and j + 3 < SLOTS)
                    if then := ahead(r, j, last, 1):
                        mask_step(*then, first and j + 1 < SLOTS, range(1))
                    upper_step(r, j, first)
                    form_step(r, j, first)
                    if then:
                        mask_step(*then, first and j + 1 < SLOTS, range(1, PICKS[then[1]]))
                    if first and j == 2:
                        dve.wait_ge(s_turned, turns_before(layer) + NBLOCKS)
                    if j >= 2:
                        add_step(r, j - 2, first, base_of(r * SLOTS + j - 2))
                    elif not first:
                        add_step(r - 1, j - 2 + SLOTS, False, base_of(r * SLOTS + j - 2))
                    if then:
                        picked_step(*then)

                dve.wait_ge(s_code_steps, 6)
                for j in range(3):
                    hot_step(0, j, True)
                mask_step(0, 0, True, range(PICKS[0]))
                picked_step(0, 0)
                rounds(dve, step)
                for j in (SLOTS - 2, SLOTS - 1):
                    add_step(ROUNDS - 1, j, False, base_of((ROUNDS - 1) * SLOTS + j))
                dve.wait_ge(s_add, done + CHUNKS)

                v.tensor_scalar(iota_w[:], iota[:], float(WINDOW - WIDE), None, ALU.add).then_inc(w_iota, 1)
                dve.sem_inc(w_add, 1)

                def window(w):
                    taken(dve, w_iota, 1)
                    v.tensor_scalar(iota_w[:], iota_w[:], float(WIDE), None, ALU.add).then_inc(w_iota, 1)

                def chunk(w, c):
                    dve.sem_inc(w_go_sp, 1)
                    dve.sem_inc(w_go_pool, 1)
                    dve.wait_ge(w_iota, 1)
                    one_hots(wide_hot, c, iota_w[:], WIDE).then_inc(w_form, 1)
                    taken(dve, w_attr, 16)
                    taken(dve, w_rows, 1)
                    v.tensor_copy(h_parts[0][:, :, 0, :], h_src[0][:]).then_inc(w_high, 1)
                    products(0)
                    taken(dve, w_high, 1)
                    lower_part(0).then_inc(w_form, 1)
                    base = nc.values_load(base_i[0:1, bass.ds(c, 1)], engines=(DVE,), min_val=0,
                                          max_val=N - 1, skip_runtime_bounds_check_because="a node's number")
                    start = dve.snap(base + w * WIDE + WINDOW)
                    clamped = nc.s_assert_within(start - (start - N) * (start > N), 0, N,
                                                 skip_runtime_bounds_check_because="cut off at N")
                    taken(dve, w_agg, 1)
                    at = nodes[:, bass.ds(clamped, WIDE)]
                    taken(dve, w_add, 1)
                    v.tensor_tensor(at, at, ps_g[0:D, 2, :], ALU.add).then_inc(w_add, 1)
                    dve.wait_ge(w_add, 1)

                further_windows(dve, DVE, Body(window, chunk))
                taken(dve, w_iota, 1)
                taken(dve, w_add, 1)
                dve.sem_inc(s_whole, 1)

                if layer < LAYERS - 1:
                    for b in range(NBLOCKS):
                        v.bn_stats(bn_parts[:, b, :], nodes[:, b * NB:(b + 1) * NB]).then_inc(s_bn, 1)
                    before = layer * (NBLOCKS + 2)
                    dve.wait_ge(s_bn, before + NBLOCKS)
                    v.bn_aggr(bn_mv[:], bn_parts[:].rearrange("q b s -> q (b s)")).then_inc(s_bn, 1)
                    dve.wait_ge(s_bn, before + NBLOCKS + 1)
                    v.tensor_scalar(bn_s[:, 0:1], bn_mv[:, 1:2], BN_EPS, None, ALU.add).then_inc(s_bn, 1)
                    dve.wait_ge(s_bn_std, layer + 1)
                    v.reciprocal(bn_s[:, 2:3], bn_s[:, 1:2]).then_inc(s_bn_done, 1)
                    dve.wait_ge(s_bn_done, 4 * layer + 1)
                    v.tensor_tensor(bn_s[:, 2:3], bn_s[:, 2:3], gamma[:, layer:layer + 1], ALU.mult).then_inc(s_bn_done, 1)
                    dve.wait_ge(s_bn_done, 4 * layer + 2)
                    v.tensor_tensor(bn_s[:, 3:4], bn_mv[:, 0:1], bn_s[:, 2:3], ALU.mult).then_inc(s_bn_done, 1)
                    dve.wait_ge(s_bn_done, 4 * layer + 3)
                    v.tensor_tensor(bn_s[:, 3:4], beta[:, layer:layer + 1], bn_s[:, 3:4], ALU.subtract).then_inc(s_bn_done, 1)

            dve.wait_ge(s_table, 16 * LAYERS)
            for k in range(TURNS_OUT):
                n = turns_before(LAYERS - 1) + NBLOCKS + k
                dve.wait_ge(s_turn, n + 1)
                rows = h_rows[:, k * PER_R:(k + 1) * PER_R, :]
                v.tensor_tensor(rows, ps_n[0:ROWS, n % 2, 0:PER_R * D].rearrange("p (j d) -> p j d", d=D),
                                b_pred[:].unsqueeze(1).to_broadcast([ROWS, PER_R, D]), ALU.add).then_inc(s_fin, 1)
                dve.wait_ge(s_fin, 2 * k + 1)
                v.tensor_tensor(rows, rows, x_rows[:, k * PER_R:(k + 1) * PER_R, :], ALU.add).then_inc(s_fin, 1)


def kernel(**inputs):
    import numpy as np
    import concourse.bacc as bacc
    from concourse.bass_utils import run_bass_kernel_spmd

    def edges_by_chunk(a):
        return np.ascontiguousarray(np.asarray(a).reshape(-1, P, TILES * (a.shape[1] if a.ndim > 1 else 1)))

    arrays = {
        "x": inputs["x"],
        "src": edges_by_chunk(inputs["src"]),
        "src_rows": np.asarray(inputs["src"]).reshape(-1, P, TILES)[:, :, :PICKED].transpose(0, 2, 1)
                      .reshape(-1, PICKED * P),
        "src_cols": np.asarray(inputs["src"]).reshape(-1, P, TILES)[:, :, :PICKED].transpose(1, 0, 2),
        "dst": np.asarray(inputs["dst"]).reshape(-1, P, TILES).transpose(1, 0, 2),
        "edge_attr": edges_by_chunk(inputs["edge_attr_8"]),
        "edge_w": inputs["L0_gnn_edge_w"],
        "edge_b": inputs["L0_gnn_edge_b"],
        "root_w": inputs["L0_gnn_root_w"],
        "root_bt": np.asarray(inputs["L0_gnn_root_b"]).T,
        "gamma_t": np.asarray(inputs["L0_gnn_bn_gamma"]).T,
        "beta_t": np.asarray(inputs["L0_gnn_bn_beta"]).T,
        "pred_w": inputs["L0_gnn_pred_w"],
        "pred_b": np.asarray(inputs["L0_gnn_pred_b"]).reshape(1, -1),
    }
    arrays = {f"in_{k}": np.ascontiguousarray(a) for k, a in arrays.items()}
    nc = bacc.Bacc("TRN2", target_bir_lowering=False, num_devices=1)
    args = [nc.dram_tensor(k, a.shape, mybir.dt.from_np(a.dtype), kind="ExternalInput").ap()
            for k, a in arrays.items()]
    out = nc.dram_tensor("out", inputs["x"].shape, F32, kind="ExternalOutput").ap()
    gnn(nc, *args, out)
    r = run_bass_kernel_spmd(nc, [arrays], core_ids=[0])
    return r.results[0]["out"]
```
